# Optimizing a Trainium2 kernel written in Bass

```python
import numpy as np
import jax
import jax.numpy as jnp

def _softmax(x, axis=-1):
    return jax.nn.softmax(x, axis=axis)

def _gelu(x):
    return jax.nn.gelu(x, approximate=True)

def _silu(x):
    return jax.nn.silu(x)

def _sigmoid(x):
    return jax.nn.sigmoid(x)

def _layernorm(x, axis=-1, eps=1e-05):
    m = jnp.mean(x, axis=axis, keepdims=True)
    v = jnp.var(x, axis=axis, keepdims=True)
    return (x - m) / jnp.sqrt(v + eps)

def _scatter_add(tgt, idx, src, axis=0):
    return tgt.at[idx].add(src)

def _segment_sum(src, seg, n):
    return jax.ops.segment_sum(src, seg, n)
kernel_name = 'mk_adaln_d1_jaxref_r8_9a4510'

def setup_inputs(seed: int=0):
    np.random.seed(seed)
    _w = jnp.asarray

    def _L0_attn_setup():
        import jax, jax.numpy as jnp
        import numpy as np
        D_MODEL = 128
        D_HEAD = 64
        EPS = 1e-06

        def _forward(x, norm_w, Wq, Wk, Wv, wi_w, wi_b, wf_w, wf_b, Wo, bo, Wout):
            B, T, d_model = x.shape
            d = Wq.shape[0]
            scale = 1.0 / jnp.sqrt(jnp.asarray(d, x.dtype))
            normed = x * jax.lax.rsqrt(jnp.mean(x * x, axis=-1, keepdims=True) + EPS) * norm_w
            q = jnp.einsum('btm,dm->btd', normed, Wq) * scale
            k = jnp.einsum('btm,dm->btd', normed, Wk) * scale
            v = jnp.einsum('btm,dm->btd', normed, Wv)
            zi = jnp.einsum('btm,m->bt', normed, wi_w[0]) + wi_b[0]
            zf = jnp.einsum('btm,m->bt', normed, wf_w[0]) + wf_b[0]
            o = jax.nn.sigmoid(jnp.einsum('btm,dm->btd', normed, Wo) + bo)
            qT = jnp.moveaxis(q, 1, 0)
            kT = jnp.moveaxis(k, 1, 0)
            vT = jnp.moveaxis(v, 1, 0)
            ziT = jnp.moveaxis(zi, 1, 0)
            zfT = jnp.moveaxis(zf, 1, 0)
            oT = jnp.moveaxis(o, 1, 0)
            C0 = jnp.zeros((B, d, d), x.dtype)
            n0 = jnp.zeros((B, d), x.dtype)
            m0 = jnp.full((B,), -jnp.inf, x.dtype)

            def step(carry, inp):
                C, n, m = carry
                q_t, k_t, v_t, zi_t, zf_t, o_t = inp
                m_t = jnp.maximum(zf_t + m, zi_t)
                i_p = jnp.exp(zi_t - m_t)
                f_p = jnp.exp(zf_t + m - m_t)
                C_t = f_p[:, None, None] * C + i_p[:, None, None] * (v_t[:, :, None] * k_t[:, None, :])
                n_t = f_p[:, None] * n + i_p[:, None] * k_t
                Cq = jnp.einsum('bij,bj->bi', C_t, q_t)
                denom = jnp.maximum(jnp.abs(jnp.sum(n_t * q_t, axis=-1, keepdims=True)), 1.0)
                h = o_t * Cq / denom
                return ((C_t, n_t, m_t), h)
            (C_f, n_f, m_f), hT = jax.lax.scan(step, (C0, n0, m0), (qT, kT, vT, ziT, zfT, oT))
            h = jnp.moveaxis(hT, 0, 1)
            out = x + jnp.einsum('btd,md->btm', h, Wout)
            return out
        key = jax.random.key(seed)
        ks = jax.random.split(key, 12)
        s = 0.02
        B, T = (8, 256)
        return {'x': jax.random.normal(ks[0], (B, T, D_MODEL), dtype=jnp.float32), 'norm_w': jnp.ones((D_MODEL,), dtype=jnp.float32), 'Wq': jax.random.normal(ks[1], (D_HEAD, D_MODEL), dtype=jnp.float32) * s, 'Wk': jax.random.normal(ks[2], (D_HEAD, D_MODEL), dtype=jnp.float32) * s, 'Wv': jax.random.normal(ks[3], (D_HEAD, D_MODEL), dtype=jnp.float32) * s, 'wi_w': jax.random.normal(ks[4], (1, D_MODEL), dtype=jnp.float32) * s, 'wi_b': jnp.zeros((1,), dtype=jnp.float32), 'wf_w': jax.random.normal(ks[5], (1, D_MODEL), dtype=jnp.float32) * s, 'wf_b': jnp.zeros((1,), dtype=jnp.float32), 'Wo': jax.random.normal(ks[6], (D_HEAD, D_MODEL), dtype=jnp.float32) * s, 'bo': jnp.zeros((D_HEAD,), dtype=jnp.float32), 'Wout': jax.random.normal(ks[7], (D_MODEL, D_HEAD), dtype=jnp.float32) * s}
    _L0_attn_in = _L0_attn_setup()

    def _L0_ffn_setup():
        import jax, jax.numpy as jnp
        import numpy as np
        HIDDEN = 128
        NUM_EXPERTS = 8
        TOP_K = 2
        B, S = (4, 128)
        key = jax.random.key(seed)
        ks = jax.random.split(key, 8)
        H, E = (HIDDEN, NUM_EXPERTS)
        sc = lambda fan_in: 1.0 / np.sqrt(fan_in)
        x = jax.random.normal(ks[0], (B, S, H), dtype=jnp.float32)
        Wr = jax.random.uniform(ks[1], (H, E), minval=-sc(H), maxval=sc(H), dtype=jnp.float32)
        br = jax.random.uniform(ks[2], (E,), minval=-sc(H), maxval=sc(H), dtype=jnp.float32)
        W1 = jax.random.uniform(ks[3], (E, H, 2 * H), minval=-sc(H), maxval=sc(H), dtype=jnp.float32)
        b1 = jax.random.uniform(ks[4], (E, 2 * H), minval=-sc(H), maxval=sc(H), dtype=jnp.float32)
        W2 = jax.random.uniform(ks[5], (E, 2 * H, H), minval=-sc(2 * H), maxval=sc(2 * H), dtype=jnp.float32)
        b2 = jax.random.uniform(ks[6], (E, H), minval=-sc(2 * H), maxval=sc(2 * H), dtype=jnp.float32)
        return {'x': x, 'Wr': Wr, 'br': br, 'W1': W1, 'b1': b1, 'W2': W2, 'b2': b2}
    _L0_ffn_in = _L0_ffn_setup()
    _L0_c = _w((lambda *s: np.random.randn(*s).astype(np.float32) * 0.05)(8, 128))
    _L0_wmod = _w((lambda *s: np.random.randn(*s).astype(np.float32) * 0.05)(128, 6 * 128) * 128 ** (-0.5))
    _d = {'L0_attn_x': _L0_attn_in['x'], 'L0_attn_norm_w': _L0_attn_in['norm_w'], 'L0_attn_Wq': _L0_attn_in['Wq'], 'L0_attn_Wk': _L0_attn_in['Wk'], 'L0_attn_Wv': _L0_attn_in['Wv'], 'L0_attn_wi_w': _L0_attn_in['wi_w'], 'L0_attn_wi_b': _L0_attn_in['wi_b'], 'L0_attn_wf_w': _L0_attn_in['wf_w'], 'L0_attn_wf_b': _L0_attn_in['wf_b'], 'L0_attn_Wo': _L0_attn_in['Wo'], 'L0_attn_bo': _L0_attn_in['bo'], 'L0_attn_Wout': _L0_attn_in['Wout'], 'L0_ffn_Wr': _L0_ffn_in['Wr'], 'L0_ffn_br': _L0_ffn_in['br'], 'L0_ffn_W1': _L0_ffn_in['W1'], 'L0_ffn_b1': _L0_ffn_in['b1'], 'L0_ffn_W2': _L0_ffn_in['W2'], 'L0_ffn_b2': _L0_ffn_in['b2'], 'L0_c': _L0_c, 'L0_wmod': _L0_wmod}
    _x0 = _d['L0_attn_x']
    _d['L0_attn_x'] = jax.random.normal(jax.random.fold_in(jax.random.key(seed), 1), (8, 512, 128), dtype=_x0.dtype)
    del _x0
    return _d

def reference(L0_attn_x, L0_attn_norm_w, L0_attn_Wq, L0_attn_Wk, L0_attn_Wv, L0_attn_wi_w, L0_attn_wi_b, L0_attn_wf_w, L0_attn_wf_b, L0_attn_Wo, L0_attn_bo, L0_attn_Wout, L0_ffn_Wr, L0_ffn_br, L0_ffn_W1, L0_ffn_b1, L0_ffn_W2, L0_ffn_b2, L0_c, L0_wmod):

    def _L0_attn_ref(x, norm_w, Wq, Wk, Wv, wi_w, wi_b, wf_w, wf_b, Wo, bo, Wout):
        import jax, jax.numpy as jnp
        import numpy as np
        D_MODEL = 128
        D_HEAD = 64
        EPS = 1e-06

        def _forward(x, norm_w, Wq, Wk, Wv, wi_w, wi_b, wf_w, wf_b, Wo, bo, Wout):
            B, T, d_model = x.shape
            d = Wq.shape[0]
            scale = 1.0 / jnp.sqrt(jnp.asarray(d, x.dtype))
            normed = x * jax.lax.rsqrt(jnp.mean(x * x, axis=-1, keepdims=True) + EPS) * norm_w
            q = jnp.einsum('btm,dm->btd', normed, Wq) * scale
            k = jnp.einsum('btm,dm->btd', normed, Wk) * scale
            v = jnp.einsum('btm,dm->btd', normed, Wv)
            zi = jnp.einsum('btm,m->bt', normed, wi_w[0]) + wi_b[0]
            zf = jnp.einsum('btm,m->bt', normed, wf_w[0]) + wf_b[0]
            o = jax.nn.sigmoid(jnp.einsum('btm,dm->btd', normed, Wo) + bo)
            qT = jnp.moveaxis(q, 1, 0)
            kT = jnp.moveaxis(k, 1, 0)
            vT = jnp.moveaxis(v, 1, 0)
            ziT = jnp.moveaxis(zi, 1, 0)
            zfT = jnp.moveaxis(zf, 1, 0)
            oT = jnp.moveaxis(o, 1, 0)
            C0 = jnp.zeros((B, d, d), x.dtype)
            n0 = jnp.zeros((B, d), x.dtype)
            m0 = jnp.full((B,), -jnp.inf, x.dtype)

            def step(carry, inp):
                C, n, m = carry
                q_t, k_t, v_t, zi_t, zf_t, o_t = inp
                m_t = jnp.maximum(zf_t + m, zi_t)
                i_p = jnp.exp(zi_t - m_t)
                f_p = jnp.exp(zf_t + m - m_t)
                C_t = f_p[:, None, None] * C + i_p[:, None, None] * (v_t[:, :, None] * k_t[:, None, :])
                n_t = f_p[:, None] * n + i_p[:, None] * k_t
                Cq = jnp.einsum('bij,bj->bi', C_t, q_t)
                denom = jnp.maximum(jnp.abs(jnp.sum(n_t * q_t, axis=-1, keepdims=True)), 1.0)
                h = o_t * Cq / denom
                return ((C_t, n_t, m_t), h)
            (C_f, n_f, m_f), hT = jax.lax.scan(step, (C0, n0, m0), (qT, kT, vT, ziT, zfT, oT))
            h = jnp.moveaxis(hT, 0, 1)
            out = x + jnp.einsum('btd,md->btm', h, Wout)
            return out
        return _forward(x, norm_w, Wq, Wk, Wv, wi_w, wi_b, wf_w, wf_b, Wo, bo, Wout)

    def _L0_ffn_ref(x, Wr, br, W1, b1, W2, b2):
        import jax, jax.numpy as jnp
        import numpy as np
        HIDDEN = 128
        NUM_EXPERTS = 8
        TOP_K = 2
        B, S = (4, 128)
        B_, S_, H = x.shape
        xf = x.reshape(-1, H)
        logits = xf @ Wr + br
        topk_w, topk_idx = jax.lax.top_k(logits, TOP_K)
        topk_w = jax.nn.softmax(topk_w, axis=-1)
        gate = jnp.sum(jax.nn.one_hot(topk_idx, NUM_EXPERTS, dtype=xf.dtype) * topk_w[..., None], axis=1)
        h = jax.nn.relu(jnp.einsum('th,ehf->etf', xf, W1) + b1[:, None, :])
        y = jnp.einsum('etf,efh->eth', h, W2) + b2[:, None, :]
        out = jnp.einsum('te,eth->th', gate, y)
        return out.reshape(B_, S_, H)
    x = L0_attn_x
    mod = (_silu(L0_c) @ L0_wmod).reshape(L0_c.shape[0], 6, 1, -1)
    sa, ca, ga, sb, cb, gb = (mod[:, 0], mod[:, 1], mod[:, 2], mod[:, 3], mod[:, 4], mod[:, 5])
    ga = (2 * (ga >= 0) - 1) * jnp.maximum(jnp.abs(ga), 0.25)
    gb = (2 * (gb >= 0) - 1) * jnp.maximum(jnp.abs(gb), 0.25)
    h = _layernorm(x, axis=-1) * (1 + ca) + sa
    x = x + ga * _L0_attn_ref(h, L0_attn_norm_w, L0_attn_Wq, L0_attn_Wk, L0_attn_Wv, L0_attn_wi_w, L0_attn_wi_b, L0_attn_wf_w, L0_attn_wf_b, L0_attn_Wo, L0_attn_bo, L0_attn_Wout)
    h = _layernorm(x, axis=-1) * (1 + cb) + sb
    x = x + gb * _L0_ffn_ref(h, L0_ffn_Wr, L0_ffn_br, L0_ffn_W1, L0_ffn_b1, L0_ffn_W2, L0_ffn_b2)
    return x

_drawn_inputs = setup_inputs


def setup_inputs(seed=0):
    import zlib

    import numpy as np

    out = dict(_drawn_inputs(seed))
    spreads = {'L0_attn_norm_w': (1.0, 0.6), 'L0_attn_bo': (0.0, 0.8)}
    factors = {'L0_attn_Wq': 8.0,
     'L0_attn_Wk': 8.0,
     'L0_attn_Wv': 8.0,
     'L0_attn_wi_w': 8.0,
     'L0_attn_wf_w': 8.0,
     'L0_attn_Wo': 8.0,
     'L0_attn_Wout': 8.0,
     'L0_ffn_br': 5.638,
     'L0_ffn_b1': 8.0,
     'L0_ffn_b2': 8.0}
    for name, (base, spread) in spreads.items():
        noise = np.random.default_rng([zlib.crc32(name.encode()), seed]).standard_normal(out[name].shape)
        drawn = base * np.exp(spread * noise) if base else spread * noise
        out[name] = jnp.asarray(drawn.astype(out[name].dtype))
    for name, factor in factors.items():
        out[name] = (out[name] * factor).astype(out[name].dtype)
    return out
```

```python
import concourse.bass as bass
from concourse import mybir
from contextlib import ExitStack


def adaln_mlstm_moe_kernel(
    nc: bass.Bass,
    x_in: bass.AP,
    norm_w: bass.AP,
    Wq: bass.AP,
    Wk: bass.AP,
    Wv: bass.AP,
    wi_w: bass.AP,
    wi_b: bass.AP,
    wf_w: bass.AP,
    wf_b: bass.AP,
    Wo: bass.AP,
    bo: bass.AP,
    Wout: bass.AP,
    Wr: bass.AP,
    br: bass.AP,
    W1: bass.AP,
    b1: bass.AP,
    W2: bass.AP,
    b2: bass.AP,
    c_in: bass.AP,
    wmod: bass.AP,
    out: bass.AP,
):
    fp32 = mybir.dt.float32
    fp32r = mybir.dt.float32r
    u32 = mybir.dt.uint32
    ALU = mybir.AluOpType
    ACT = mybir.ActivationFunctionType

    P = 128
    B, T, D = x_in.shape
    DH = Wq.shape[0]
    E = Wr.shape[1]
    FF = W1.shape[2]
    NT = T // P
    NU = FF // P
    N = E * NU
    NMOD = wmod.shape[1] // D
    PAIRS = B // 2
    LN_EPS, RMS_EPS = 1e-5, 1e-6
    SCALE = float(DH) ** -0.5
    FAR = 1e30
    NVO = 2 * DH + 2
    NS = DH + 1
    LO = 32
    GK = LO + E
    R_C, R_B1, R_WI, R_WF, R_NORM, R_END = 0, B, B + E * NU, B + E * NU + 1, B + E * NU + 2, B + E * NU + 3
    WIDTH = [T - P * j for j in range(NT)]
    START = [sum(WIDTH[:j]) for j in range(NT)]
    NW = sum(WIDTH)

    ctx = ExitStack()
    with ctx:
        def sb(name, shape, dt=fp32):
            return ctx.enter_context(nc.sbuf_tensor(name, shape, dt))

        def sem(name):
            return ctx.enter_context(nc.semaphore(name))

        ident = sb("ident", [P, P])
        ones = sb("ones", [P, P])
        tri = sb("tri", [P, P])
        far = sb("far", [P, P])
        mean_col = sb("mean_col", [P, 1])
        neg_row = sb("neg_row", [1, T])
        iota_e = sb("iota_e", [P, E])
        minus_half = sb("minus_half", [P, NT])
        sel_r = sb("sel_r", [GK, E, P], fp32r)
        small_rows = sb("small_rows", [R_END, D])
        qk_raw = sb("qk_raw", [2 * DH, D])
        vo_raw = sb("vo_raw", [2 * DH, D])
        wout_raw = sb("wout_raw", [D, DH])
        wmod_sb = sb("wmod_sb", [D, NMOD * D])
        w1_raw = sb("w1_raw", [D, E, FF])
        w2_raw = sb("w2_raw", [P, E, NU, D])
        b2_raw = sb("b2_raw", [GK, D])
        wr_sb = sb("wr_sb", [D, E])
        zb_bc = sb("zb_bc", [P, 2])
        bo_bc = sb("bo_bc", [P, DH])
        br_bc = sb("br_bc", [P, E])
        cols = sb("cols", [P, R_END])
        silu_c = sb("silu_c", [P, B])
        tanh_c = sb("tanh_c", [P, B])
        mods = sb("mods", [P, NMOD, B])
        sign_g = sb("sign_g", [P, 2, B])
        mag_g = sb("mag_g", [P, 2, B])
        wqk = sb("wqk", [D, 2 * DH])
        wvo = sb("wvo", [D, NVO])
        woutT = sb("woutT", [DH, D])
        diag_ga = sb("diag_ga", [P, B, D])
        wout_ga = sb("wout_ga", [DH, B, D])
        w1_hi = sb("w1_hi", [D, E, FF], fp32r)
        w1_lo = sb("w1_lo", [D, E, FF], fp32r)
        w2_hi = sb("w2_hi", [P, E, NU, D], fp32r)
        w2_lo = sb("w2_lo", [P, E, NU, D], fp32r)
        b2_hi = sb("b2_hi", [GK, D], fp32r)
        b2_lo = sb("b2_lo", [GK, D], fp32r)
        x_all = sb("x_all", [P, B * T])
        h2_hi = sb("h2_hi", [D, B * T], fp32r)
        h2_lo = sb("h2_lo", [D, B * T], fp32r)
        top_val = sb("top_val", [P, B * NT * 2])
        top_idx = sb("top_idx", [P, B * NT * 2])
        gates = sb("gates", [P, B * NT, E])
        gate_a = sb("gate_a", [P, B * NT, E])
        gate_b = sb("gate_b", [P, B * NT, E])
        top_d = sb("top_d", [P, B * NT])
        top_e2 = sb("top_e2", [P, B * NT])
        top_s = sb("top_s", [P, B * NT])
        top_g = sb("top_g", [P, 2, B * NT])
        gateT = sb("gateT", [GK, B * T], fp32r)

        def two(name, shape, dt=fp32):
            return [sb(f"{name}{p}", shape, dt) for p in range(2)]

        stats = two("stats", [P, NT, 6])
        mv = two("mv", [P, NT, 2])
        var_eps = two("var_eps", [P, NT])
        rstd = two("rstd", [P, NT])
        xn = two("xn", [P, NT, D])
        hT = two("hT", [D, T])
        sq = two("sq", [D, T])
        ms_eps = two("ms_eps", [P, NT])
        rms = two("rms", [P, NT])
        rms2 = two("rms2", [P, NT])
        rms_inv = two("rms_inv", [P, NT])
        qT = two("qT", [DH, T])
        kT = two("kT", [DH, T])
        zg = two("zg", [P, NT, 2])
        vs = two("vs", [P, NT, NS])
        zo = two("zo", [P, NT, DH])
        th = two("th", [P, NT, DH])
        a_col = two("a_col", [P, NT])
        m_row = two("m_row", [1, T])
        mb = two("mb", [P, NT, P])
        ew = two("ew", [P, NW])
        den = two("den", [P, NT])
        rden = two("rden", [P, NT])
        uh = two("uh", [P, NT, DH])
        hh = two("hh", [P, NT, DH])
        hhT = two("hhT", [DH, T])
        h2T = two("h2T", [D, T])
        lg = two("lg", [P, NT, E])
        mx = two("mx", [P, NT, 8])
        ix = two("ix", [P, NT, 8], u32)
        sel = ew[0][0:GK, 0:E * P].rearrange("k (e m) -> k e m", e=E)
        hid = [sq[0][:, :], sq[1][:, :]]
        hg = [hT[0][:, :], hT[1][:, :], xn[0][:, :, :].rearrange("p j d -> p (j d)")]
        hg_hi = [sb(f"hg_hi{k}", [P, T], fp32r) for k in range(2)]
        hg_lo = [sb(f"hg_lo{k}", [P, T], fp32r) for k in range(2)]
        y_sb = h2T[0]
        gate_blk = sb("gate_blk", [P, NT, E])

        bank = [ctx.enter_context(nc.psum_tensor(f"bank{k}", [P, 512], fp32)) for k in range(8)]
        bA, bB, bC, bD = ([bank[k], bank[4 + k]] for k in range(4))

        s_small = sem("s_small")
        s_wqkvo = sem("s_wqkvo")
        s_wmod = sem("s_wmod")
        s_bc = sem("s_bc")
        s_w1 = sem("s_w1")
        s_w2 = sem("s_w2")
        s_b2 = sem("s_b2")
        s_const = sem("s_const")
        s_pool = sem("s_pool")
        s_colsT = sem("s_colsT")
        s_wT = sem("s_wT")
        s_cols = sem("s_cols")
        s_tanhc = sem("s_tanhc")
        s_silu = sem("s_silu")
        s_mod = sem("s_mod")
        s_dve0 = sem("s_dve0")
        s_w = sem("s_w")
        s_diag = sem("s_diag")
        s_gab = sem("s_gab")
        s_ready = sem("s_ready")
        s_w12 = sem("s_w12")
        s_w12h = sem("s_w12h")
        x_loaded = [sem(f"x_loaded{p}") for p in range(2)]
        s_stats = sem("s_stats")
        s_var = sem("s_var")
        s_ve = sem("s_ve")
        s_rstd = sem("s_rstd")
        s_xn = sem("s_xn")
        s_xT = sem("s_xT")
        s_hT = sem("s_hT")
        s_sq = sem("s_sq")
        s_qk = sem("s_qk")
        s_qkT = sem("s_qkT")
        s_ms = sem("s_ms")
        s_mse = sem("s_mse")
        s_rms = sem("s_rms")
        s_rms2 = sem("s_rms2")
        s_voz = sem("s_voz")
        s_z = sem("s_z")
        s_v = sem("s_v")
        s_zo = sem("s_zo")
        s_th = sem("s_th")
        s_F = sem("s_F")
        s_a = sem("s_a")
        s_aT = sem("s_aT")
        s_M = sem("s_M")
        s_Mb = sem("s_Mb")
        s_mask = sem("s_mask")
        s_E = sem("s_E")
        s_S = sem("s_S")
        s_P = sem("s_P")
        s_pv = sem("s_pv")
        s_den = sem("s_den")
        s_rd = sem("s_rd")
        s_hh = sem("s_hh")
        s_hhT = sem("s_hhT")
        s_hhc = sem("s_hhc")
        s_x1p = sem("s_x1p")
        s_x1 = sem("s_x1")
        s_xn2 = sem("s_xn2")
        s_x2T = sem("s_x2T")
        s_h2 = sem("s_h2")
        s_h2hi = sem("s_h2hi")
        s_lo = sem("s_lo")
        s_lgp = sem("s_lgp")
        s_lg = sem("s_lg")
        s_mx = sem("s_mx")
        s_ix = sem("s_ix")
        s_top = sem("s_top")
        s_td = sem("s_td")
        s_te = sem("s_te")
        s_tc = sem("s_tc")
        s_gates = sem("s_gates")
        s_gblk = sem("s_gblk")
        s_gT = sem("s_gT")
        s_ghi = sem("s_ghi")
        s_glo = sem("s_glo")
        s_up = sem("s_up")
        s_hid = sem("s_hid")
        s_gb = sem("s_gb")
        s_hg = sem("s_hg")
        s_hghi = sem("s_hghi")
        s_hglo = sem("s_hglo")
        s_dn = sem("s_dn")
        s_ysb = sem("s_ysb")
        s_yT = sem("s_yT")
        s_o = sem("s_o")
        s_out = sem("s_out")

        block = ctx.enter_context(nc.Block())

        x_v = x_in.rearrange("b (j p) d -> b p j d", p=P)
        out_v = out.rearrange("b (j p) d -> b p j d", p=P)

        def row(ap, b):
            return ap[:, bass.ds(b * T, T)]

        def bcast(ap, n):
            return ap.unsqueeze(2).to_broadcast([ap.shape[0], ap.shape[1], n])

        def wait_apart(eng, of, value):
            value = eng.to_reg(value)
            eng.wait_ge(s_const, 16)
            eng.wait_ge(of, value)

        @block.sync
        def _(sp):
            sp.dma_start(small_rows[R_C:R_C + B, :], c_in).then_inc(s_small, 16)
            sp.dma_start(small_rows[R_B1:R_WI, :], b1.rearrange("e (u f) -> (e u) f", f=P)).then_inc(s_small, 16)
            sp.dma_start(small_rows[R_WI:R_WF, :], wi_w).then_inc(s_small, 16)
            sp.dma_start(small_rows[R_WF:R_NORM, :], wf_w).then_inc(s_small, 16)
            sp.dma_start(small_rows[R_NORM:R_END, :], norm_w.rearrange("(a n) -> a n", a=1)).then_inc(s_small, 16)
            for p in range(2):
                sp.dma_start(x_all[:, p * T:(p + 1) * T].rearrange("p (j d) -> p j d", j=NT), x_v[p]).then_inc(x_loaded[p], 16)
            with sp.Fori(1, PAIRS) as i:
                for p in range(2):
                    sp.wait_ge(x_loaded[p], i * 16)
                    sp.dma_start(row(x_all, i * 2 + p).rearrange("p (j d) -> p j d", j=NT),
                                 x_v[bass.ds(i * 2 + p, 1)].rearrange("b p j d -> p (b j) d")).then_inc(x_loaded[p], 16)
            with sp.Fori(0, B) as b:
                sp.wait_ge(s_o, b + 1)
                sp.dma_start(out_v[bass.ds(b, 1)].rearrange("b p j d -> p (b j) d"),
                             row(x_all, b).rearrange("p (j d) -> p j d", j=NT)).then_inc(s_out, 16)
            sp.wait_ge(s_out, 16 * B)

        @block.gpsimd
        def _(pool):
            g = nc.gpsimd
            g.memset(ident[:, :], 0.0).then_inc(s_pool, 1)
            g.memset(tri[:, :], 1.0).then_inc(s_pool, 1)
            g.memset(far[:, :], 0.0).then_inc(s_pool, 1)
            g.memset(sel, 0.0).then_inc(s_pool, 1)
            g.memset(ones[:, :], 1.0).then_inc(s_const, 1)
            g.memset(mean_col[:, :], 1.0 / D).then_inc(s_const, 1)
            g.memset(neg_row[:, :], -3e38).then_inc(s_const, 1)
            g.memset(minus_half[:, :], -0.5).then_inc(s_const, 1)
            for e in range(E):
                g.memset(iota_e[:, e:e + 1], float(e)).then_inc(s_const, 1)
            pool.wait_ge(s_pool, 4)
            g.affine_select(out=ident[:, :], in_=ident[:, :], compare_op=ALU.not_equal, fill=1.0, base=0,
                            pattern=[[-1, P]], channel_multiplier=1).then_inc(s_const, 1)
            g.affine_select(out=tri[:, :], in_=tri[:, :], compare_op=ALU.is_ge, fill=0.0, base=0,
                            pattern=[[1, P]], channel_multiplier=-1).then_inc(s_const, 1)
            g.affine_select(out=far[:, :], in_=far[:, :], compare_op=ALU.is_ge, fill=FAR, base=0,
                            pattern=[[1, P]], channel_multiplier=-1).then_inc(s_const, 1)
            g.affine_select(out=sel, in_=sel, compare_op=ALU.not_equal, fill=1.0, base=0,
                            pattern=[[-1, E], [0, P]], channel_multiplier=1).then_inc(s_pool, 1)
            pool.wait_ge(s_pool, 5)
            g.affine_select(out=sel, in_=sel, compare_op=ALU.not_equal, fill=1.0, base=-LO,
                            pattern=[[-1, E], [0, P]], channel_multiplier=1).then_inc(s_const, 1)
            pool.wait_ge(s_const, 16)

            with pool.Fori(0, PAIRS) as i:
                for p in range(2):
                    pool.wait_ge(s_ve, i * 4 + (p + 1))
                    g.tensor_tensor(rstd[p][:, :], var_eps[p][:, :], minus_half[:, :], ALU.pow).then_inc(s_rstd, 1)
                for p in range(2):
                    pool.wait_ge(s_mse, i * 2 + (p + 1))
                    g.tensor_tensor(rms[p][:, :], ms_eps[p][:, :], minus_half[:, :], ALU.pow).then_inc(s_rms, 1)
                for p in range(2):
                    pool.wait_ge(s_ve, i * 4 + (p + 3))
                    g.tensor_tensor(rstd[p][:, :], var_eps[p][:, :], minus_half[:, :], ALU.pow).then_inc(s_rstd, 1)
                for p in range(2):
                    pool.wait_ge(s_h2, i * 2 + (p + 1))
                    pool.wait_ge(s_h2hi, i * 2 + (p + 1))
                    g.tensor_tensor(row(h2_lo, i * 2 + p), h2T[p][:, :], row(h2_hi, i * 2 + p).bitcast(fp32),
                                    ALU.subtract).then_inc(s_lo, 1)

        @block.scalar
        def _(act):
            a = nc.scalar
            act.dma_start(wmod_sb[:, :], wmod).then_inc(s_wmod, 16)
            act.dma_start(qk_raw[0:DH, :], Wq).then_inc(s_wqkvo, 16)
            act.dma_start(qk_raw[DH:2 * DH, :], Wk).then_inc(s_wqkvo, 16)
            act.dma_start(vo_raw[0:DH, :], Wv).then_inc(s_wqkvo, 16)
            act.dma_start(vo_raw[DH:2 * DH, :], Wo).then_inc(s_wqkvo, 16)
            act.dma_start(wout_raw[:, :], Wout).then_inc(s_wqkvo, 16)
            act.dma_start(zb_bc[:, 0:1], wi_b.partition_broadcast(P)).then_inc(s_bc, 16)
            act.dma_start(zb_bc[:, 1:2], wf_b.partition_broadcast(P)).then_inc(s_bc, 16)
            act.dma_start(bo_bc[:, :], bo.partition_broadcast(P)).then_inc(s_bc, 16)
            act.dma_start(br_bc[:, :], br.partition_broadcast(P)).then_inc(s_bc, 16)
            act.dma_start(wr_sb[:, :], Wr).then_inc(s_bc, 16)
            act.dma_start(w1_raw[:, :, :], W1.rearrange("e h f -> h e f")).then_inc(s_w1, 16)
            act.dma_start(w2_raw[:, :, :, :].rearrange("f e u h -> f (e u) h"),
                          W2.rearrange("e (u f) h -> f (e u) h", f=P)).then_inc(s_w2, 16)
            act.dma_start(b2_raw[0:E, :], b2).then_inc(s_b2, 16)
            act.dma_start(b2_raw[LO:LO + E, :], b2).then_inc(s_b2, 16)
            act.wait_ge(s_cols, 1)
            a.activation(tanh_c[:, :], cols[:, R_C:R_C + B], ACT.Tanh, scale=0.5).then_inc(s_tanhc, 1)

            with act.Fori(0, PAIRS) as i:
                for p in range(2):
                    b = i * 2 + p
                    act.wait_ge(s_xT, b + 1)
                    sa, ca = mods[:, 0, bass.ds(b, 1)], mods[:, 1, bass.ds(b, 1)]
                    if p == 0:
                        act.wait_ge(s_ready, 3)
                    a.activation(hT[p][:, :], bA[p][:, :], ACT.Identity, bias=sa, scale=ca).then_inc(s_hT, 1)
                    a.activation(sq[p][:, :], bA[p][:, :], ACT.Square, bias=sa, scale=ca).then_inc(s_sq, 1)
                for p in range(2):
                    b = i * 2 + p
                    act.wait_ge(s_qk, b + 1)
                    a.activation(qT[p][:, :], bB[p][0:DH, :], ACT.Copy)
                    a.activation(kT[p][:, :], bB[p][DH:2 * DH, :], ACT.Copy).then_inc(s_qkT, 1)
                for p in range(2):
                    act.wait_ge(s_zo, i * 2 + (p + 1))
                    a.activation(th[p][:, :, :], zo[p][:, :, :], ACT.Tanh, scale=0.5).then_inc(s_th, 1)
                for p in range(2):
                    b = i * 2 + p
                    act.wait_ge(s_mask, b + 1)
                    for j in range(NT):
                        last = a.activation(ew[p][:, START[j]:START[j] + P], mb[p][:, j, :], ACT.Exp,
                                            bias=a_col[p][:, j:j + 1], scale=-1.0)
                        if j < NT - 1:
                            last = a.activation(ew[p][:, START[j] + P:START[j] + WIDTH[j]], bB[p][:, P * (j + 1):T],
                                                ACT.Exp, bias=a_col[p][:, j:j + 1], scale=-1.0)
                        last.then_inc(s_E, 1)
                for p in range(2):
                    act.wait_ge(s_hhT, i * 2 + (p + 1))
                    a.activation(hhT[p][:, :], bB[p][0:DH, :], ACT.Copy).then_inc(s_hhc, 1)
                for p in range(2):
                    b = i * 2 + p
                    act.wait_ge(s_x2T, b + 1)
                    sb_, cb = mods[:, 3, bass.ds(b, 1)], mods[:, 4, bass.ds(b, 1)]
                    a.activation(h2T[p][:, :], bA[p][:, :], ACT.Identity, bias=sb_, scale=cb).then_inc(s_h2, 1)
                    a.activation(row(h2_hi, b), bA[p][:, :], ACT.Identity, bias=sb_, scale=cb).then_inc(s_h2hi, 1)

            act.wait_ge(s_td, 1)
            a.activation(top_e2[:, :], top_d[:, :], ACT.Exp).then_inc(s_te, 1)

            with act.Fori(0, B) as b:
                act.wait_ge(s_gT, b + 1)
                a.activation(row(gateT, b)[0:E, :], bank[7][0:E, :], ACT.Copy).then_inc(s_ghi, 1)
                for n in range(N):
                    act.wait_ge(s_up, b * N + (n + 1))
                    if n >= 2:
                        act.wait_ge(s_hg, b * N + (n - 1))
                    a.activation(hid[n % 2], bank[n % 2][:, :], ACT.Relu,
                                 bias=cols[:, R_B1 + n:R_B1 + n + 1]).then_inc(s_hid, 1)
                    if n >= 1:
                        act.wait_ge(s_hg, b * N + n)
                        if n >= 3:
                            act.wait_ge(s_dn, b * N + (n - 2))
                        a.activation(hg_hi[(n - 1) % 2][:, :], hg[(n - 1) % 3], ACT.Copy).then_inc(s_hghi, 1)
                act.wait_ge(s_hg, (b + 1) * N)
                act.wait_ge(s_dn, (b + 1) * N - 2)
                a.activation(hg_hi[1][:, :], hg[(N - 1) % 3], ACT.Copy).then_inc(s_hghi, 1)
                act.wait_ge(s_dn, (b + 1) * N)
                a.activation(y_sb[:, :], bank[5][:, :], ACT.Copy, scale=mods[:, 5, bass.ds(b, 1)]).then_inc(s_ysb, 1)

        @block.vector
        def _(dve):
            v = nc.vector
            dve.wait_ge(s_colsT, 1)
            v.tensor_copy(cols[:, :], bank[0][:, 0:R_END]).then_inc(s_cols, 1)
            dve.wait_ge(s_tanhc, 1)
            v.scalar_tensor_tensor(silu_c[:, :], tanh_c[:, :], 1.0, cols[:, R_C:R_C + B], ALU.add, ALU.mult).then_inc(s_silu, 1)
            dve.wait_ge(s_wT, 1)
            nw = cols[:, R_NORM:R_NORM + 1]
            v.tensor_scalar(wqk[:, :], bank[1][:, 0:2 * DH], nw, SCALE, ALU.mult, ALU.mult)
            v.tensor_scalar(wvo[:, 0:2 * DH], bank[2][:, 0:2 * DH], nw, None, ALU.mult)
            v.tensor_scalar(wvo[:, 2 * DH:NVO], cols[:, R_WI:R_WF + 1], nw, None, ALU.mult)
            v.tensor_copy(woutT[:, :], bank[3][0:DH, 0:D]).then_inc(s_ready, 1)
            dve.wait_ge(s_mod, 1)
            md = bank[4][:, 0:NMOD * B].rearrange("p (m b) -> p m b", m=NMOD)
            for m in (0, 3):
                v.tensor_scalar(mods[:, m, :], md[:, m, :], 0.5, None, ALU.mult)
                v.tensor_scalar(mods[:, m + 1, :], md[:, m + 1, :], 0.5, 1.0, ALU.mult, ALU.add)
            for n, m in enumerate((2, 5)):
                v.tensor_scalar(sign_g[:, n, :], md[:, m, :], 0.0, 1.0, ALU.is_ge, ALU.mult)
                v.tensor_scalar(mods[:, m, :], md[:, m, :], 0.5, 0.25, ALU.mult, ALU.max)
                last = v.tensor_scalar(mag_g[:, n, :], md[:, m, :], -0.5, 0.25, ALU.mult, ALU.max)
            last.then_inc(s_dve0, 1)
            dve.wait_ge(s_dve0, 1)
            v.tensor_scalar(sign_g[:, :, :], sign_g[:, :, :], 2.0, -1.0, ALU.mult, ALU.add)
            v.tensor_tensor(mag_g[:, 0, :], mag_g[:, 0, :], mods[:, 2, :], ALU.max)
            v.tensor_tensor(mag_g[:, 1, :], mag_g[:, 1, :], mods[:, 5, :], ALU.max).then_inc(s_dve0, 1)
            dve.wait_ge(s_dve0, 2)
            v.tensor_tensor(mods[:, 2, :], sign_g[:, 0, :], mag_g[:, 0, :], ALU.mult)
            v.tensor_tensor(mods[:, 5, :], sign_g[:, 1, :], mag_g[:, 1, :], ALU.mult).then_inc(s_dve0, 1)
            dve.wait_ge(s_dve0, 3)
            dve.wait_ge(s_const, 16)
            v.tensor_tensor(diag_ga[:, :, :], ident[:, :].unsqueeze(1).to_broadcast([P, B, D]),
                            bcast(mods[:, 2, :], D), ALU.mult).then_inc(s_diag, 1)
            dve.wait_ge(s_gab, 1)
            for n in range(2):
                v.scalar_tensor_tensor(wout_ga[:, 4 * n:4 * n + 4, :],
                                       bank[5 + n][0:DH, :].rearrange("p (b d) -> p b d", b=4), 0.5,
                                       woutT[:, :].unsqueeze(1).to_broadcast([DH, 4, D]),
                                       ALU.mult, ALU.mult).then_inc(s_ready, 1)
            v.tensor_copy(sel_r[:, :, :], sel).then_inc(s_w, 1)
            v.memset(y_sb[:, :], 0.0).then_inc(s_ysb, 1)
            v.memset(gateT[:, :].bitcast(fp32), 0.0).then_inc(s_w, 1)
            dve.wait_ge(s_w1, 16)
            v.tensor_copy(w1_hi[:, :, :], w1_raw[:, :, :]).then_inc(s_w12h, 1)
            dve.wait_ge(s_w2, 16)
            v.tensor_copy(w2_hi[:, :, :, :], w2_raw[:, :, :, :]).then_inc(s_w12h, 1)
            v.memset(b2_hi[:, :].bitcast(fp32), 0.0).then_inc(s_w12h, 1)
            v.memset(b2_lo[:, :].bitcast(fp32), 0.0).then_inc(s_w12h, 1)
            dve.wait_ge(s_w12h, 4)
            dve.wait_ge(s_b2, 32)
            v.tensor_copy(b2_hi[0:E, :], b2_raw[0:E, :]).then_inc(s_w12h, 1)
            v.tensor_copy(b2_hi[LO:LO + E, :], b2_raw[LO:LO + E, :]).then_inc(s_w12h, 1)
            v.tensor_tensor(w1_lo[:, :, :], w1_raw[:, :, :], w1_hi[:, :, :].bitcast(fp32), ALU.subtract).then_inc(s_w12, 1)
            v.tensor_tensor(w2_lo[:, :, :, :], w2_raw[:, :, :, :], w2_hi[:, :, :, :].bitcast(fp32), ALU.subtract).then_inc(s_w12, 1)
            dve.wait_ge(s_w12h, 6)
            v.tensor_tensor(b2_lo[0:E, :], b2_raw[0:E, :], b2_hi[0:E, :].bitcast(fp32), ALU.subtract).then_inc(s_w12, 1)
            dve.wait_ge(s_bc, 80)
            dve.wait_ge(s_w, 2)

            def stats_of(b, p, n_stats):
                for j in range(NT):
                    last = v.bn_stats(stats[p][:, j, :], x_all[:, bass.ds(b * T + j * P, P)])
                last.then_inc(s_stats, 1)
                wait_apart(dve, s_stats, n_stats)
                for j in range(NT):
                    last = v.bn_aggr(mv[p][:, j, :], stats[p][:, j, :])
                last.then_inc(s_var, 1)
                dve.wait_ge(s_var, n_stats)
                v.tensor_scalar(var_eps[p][:, :], mv[p][:, :, 1], LN_EPS, None, ALU.add).then_inc(s_ve, 1)

            def normalise(b, p, n_rstd, done):
                dve.wait_ge(s_rstd, n_rstd)
                for j in range(NT):
                    last = v.tensor_scalar(xn[p][:, j, :], x_all[:, bass.ds(b * T + j * P, P)],
                                           mv[p][:, j, 0:1], rstd[p][:, j:j + 1], ALU.subtract, ALU.mult)
                last.then_inc(done, 1)

            with dve.Fori(0, PAIRS) as i:
                for p in range(2):
                    wait_apart(dve, x_loaded[p], (i + 1) * 16)
                    stats_of(i * 2 + p, p, i * 4 + (p + 1))
                for p in range(2):
                    normalise(i * 2 + p, p, i * 4 + (p + 1), s_xn)
                for p in range(2):
                    dve.wait_ge(s_ms, i * 2 + (p + 1))
                    v.tensor_scalar(ms_eps[p][:, :], bA[p][:, 0:NT], RMS_EPS, None, ALU.add).then_inc(s_mse, 1)
                for p in range(2):
                    b = i * 2 + p
                    dve.wait_ge(s_rms, b + 1)
                    v.tensor_tensor(rms2[p][:, :], rms[p][:, :], rms[p][:, :], ALU.mult).then_inc(s_rms2, 1)
                    v.reciprocal(rms_inv[p][:, :], rms[p][:, :])
                    v.tensor_copy(vs[p][:, :, DH], rms[p][:, :])
                    dve.wait_ge(s_voz, b + 1)
                    for j in range(NT):
                        o = NVO * (j % 2)
                        src = (bC, bD)[j // 2][p]
                        last = v.scalar_tensor_tensor(zg[p][:, j, :], src[:, o + 2 * DH:o + NVO], rms[p][:, j:j + 1],
                                                      zb_bc[:, :], ALU.mult, ALU.add)
                    last.then_inc(s_z, 1)
                    for j in range(NT):
                        o = NVO * (j % 2)
                        src = (bC, bD)[j // 2][p]
                        last = v.scalar_tensor_tensor(zo[p][:, j, :], src[:, o + DH:o + 2 * DH], rms[p][:, j:j + 1],
                                                      bo_bc[:, :], ALU.mult, ALU.add)
                    last.then_inc(s_zo, 1)
                    dve.wait_ge(s_rms2, b + 1)
                    for h in range(2):
                        src = (bC, bD)[h][p][:, 0:2 * NVO].rearrange("p (j n) -> p j n", j=2)[:, :, 0:DH]
                        last = v.tensor_tensor(vs[p][:, 2 * h:2 * h + 2, 0:DH], src, bcast(rms2[p][:, 2 * h:2 * h + 2], DH), ALU.mult)
                    last.then_inc(s_v, 1)
                for p in range(2):
                    dve.wait_ge(s_F, i * 2 + (p + 1))
                    v.tensor_tensor(a_col[p][:, :], zg[p][:, :, 0], bA[p][:, 8:8 + NT], ALU.subtract).then_inc(s_a, 1)
                for p in range(2):
                    dve.wait_ge(s_aT, i * 2 + (p + 1))
                    v.tensor_tensor_scan(m_row[p][0:1, :], bA[p][0:1, :], neg_row[0:1, :], -3e38, ALU.max, ALU.max).then_inc(s_M, 1)
                for p in range(2):
                    dve.wait_ge(s_Mb, i * 2 + (p + 1))
                    v.tensor_tensor(mb[p][:, :, :], bB[p][:, :].rearrange("p (j t) -> p j t", j=NT),
                                    far[:, :].unsqueeze(1).to_broadcast([P, NT, P]), ALU.add).then_inc(s_mask, 1)
                for p in range(2):
                    b = i * 2 + p
                    for j, src in ((0, bC[p][:, 0:T]), (1, bD[p][:, 0:WIDTH[1]]),
                                   (2, bA[p][:, 0:WIDTH[2]]), (3, bD[p][:, WIDTH[1]:T])):
                        dve.wait_ge(s_E, b * NT + (j + 1))
                        dve.wait_ge(s_S, b * NT + (4 if j == 2 else 1 if j == 0 else 3))
                        w = ew[p][:, START[j]:START[j] + WIDTH[j]]
                        v.tensor_tensor(w, w, src, ALU.mult).then_inc(s_P, 1)
                for p in range(2):
                    b = i * 2 + p
                    dve.wait_ge(s_pv, b + 1)
                    pv = bC[p][:, 0:NT * NS].rearrange("p (j n) -> p j n", j=NT)
                    v.tensor_tensor(den[p][:, :], pv[:, :, DH], rms_inv[p][:, :], ALU.max).then_inc(s_den, 1)
                    dve.wait_ge(s_th, b + 1)
                    v.scalar_tensor_tensor(uh[p][:, :, :], th[p][:, :, :], 1.0, pv[:, :, 0:DH], ALU.add, ALU.mult)
                    dve.wait_ge(s_den, b * 2 + 1)
                    v.scalar_tensor_tensor(den[p][:, :], pv[:, :, DH], -1.0, den[p][:, :], ALU.mult, ALU.max).then_inc(s_den, 1)
                    dve.wait_ge(s_den, b * 2 + 2)
                    v.reciprocal(rden[p][:, :], den[p][:, :]).then_inc(s_rd, 1)
                    dve.wait_ge(s_rd, b + 1)
                    v.tensor_tensor(hh[p][:, :, :], uh[p][:, :, :], bcast(rden[p][:, :], DH), ALU.mult).then_inc(s_hh, 1)
                for p in range(2):
                    b = i * 2 + p
                    dve.wait_ge(s_x1p, b + 1)
                    v.tensor_tensor(row(x_all, b), row(x_all, b), bD[p][:, :], ALU.add).then_inc(s_x1, 1)
                    wait_apart(dve, s_x1, b + 1)
                    stats_of(b, p, i * 4 + (p + 3))
                for p in range(2):
                    normalise(i * 2 + p, p, i * 4 + (p + 3), s_xn2)
                for p in range(2):
                    b = i * 2 + p
                    dve.wait_ge(s_lgp, b + 1)
                    v.tensor_tensor(lg[p][:, :, :], bB[p][:, 0:NT * E].rearrange("p (j e) -> p j e", j=NT),
                                    br_bc[:, :].unsqueeze(1).to_broadcast([P, NT, E]), ALU.add).then_inc(s_lg, 1)
                    wait_apart(dve, s_lg, b + 1)
                    for j in range(NT):
                        last = v.max(mx[p][:, j, :], lg[p][:, j, :])
                    last.then_inc(s_mx, 1)
                    wait_apart(dve, s_mx, b + 1)
                    for j in range(NT):
                        last = v.max_index(ix[p][:, j, :], mx[p][:, j, :], lg[p][:, j, :])
                    last.then_inc(s_ix, 1)
                    v.tensor_copy(top_val[:, bass.ds(b * (NT * 2), NT * 2)].rearrange("p (j n) -> p j n", n=2), mx[p][:, :, 0:2])
                    dve.wait_ge(s_ix, b + 1)
                    v.tensor_copy(top_idx[:, bass.ds(b * (NT * 2), NT * 2)].rearrange("p (j n) -> p j n", n=2), ix[p][:, :, 0:2]).then_inc(s_top, 1)

            dve.wait_ge(s_top, B)
            tv = top_val[:, :].rearrange("p (j n) -> p j n", n=2)
            ti = top_idx[:, :].rearrange("p (j n) -> p j n", n=2)
            NJ = B * NT
            iota_b = iota_e[:, :].unsqueeze(1).to_broadcast([P, NJ, E])
            v.tensor_tensor(top_d[:, :], tv[:, :, 1], tv[:, :, 0], ALU.subtract).then_inc(s_td, 1)
            v.tensor_tensor(gate_a[:, :, :], iota_b, ti[:, :, 0:1].to_broadcast([P, NJ, E]), ALU.is_equal)
            v.tensor_tensor(gate_b[:, :, :], iota_b, ti[:, :, 1:2].to_broadcast([P, NJ, E]), ALU.is_equal)
            dve.wait_ge(s_te, 1)
            v.tensor_scalar(top_s[:, :], top_e2[:, :], 1.0, None, ALU.add).then_inc(s_tc, 1)
            dve.wait_ge(s_tc, 1)
            v.reciprocal(top_g[:, 0, :], top_s[:, :]).then_inc(s_tc, 1)
            dve.wait_ge(s_tc, 2)
            v.tensor_tensor(top_g[:, 1, :], top_g[:, 0, :], top_e2[:, :], ALU.mult).then_inc(s_tc, 1)
            v.tensor_tensor(gate_a[:, :, :], gate_a[:, :, :], bcast(top_g[:, 0, :], E), ALU.mult)
            dve.wait_ge(s_tc, 3)
            v.tensor_tensor(gate_b[:, :, :], gate_b[:, :, :], bcast(top_g[:, 1, :], E), ALU.mult).then_inc(s_tc, 1)
            dve.wait_ge(s_tc, 4)
            v.tensor_tensor(gates[:, :, :], gate_a[:, :, :], gate_b[:, :, :], ALU.add).then_inc(s_gates, 1)

            dve.wait_ge(s_gates, 1)
            with dve.Fori(0, B) as b:
                v.tensor_copy(gate_blk[:, :, :].rearrange("p j e -> p (j e)"),
                              gates[:, :, :].rearrange("p j e -> p (j e)")[:, bass.ds(b * (NT * E), NT * E)]).then_inc(s_gblk, 1)
                dve.wait_ge(s_ghi, b + 1)
                v.tensor_tensor(row(gateT, b)[LO:LO + E, :], bank[7][0:E, :], row(gateT, b)[0:E, :].bitcast(fp32),
                                ALU.subtract).then_inc(s_glo, 1)
                for n in range(N):
                    e = n // NU
                    dve.wait_ge(s_gb, b * E + (e + 1))
                    dve.wait_ge(s_hid, b * N + (n + 1))
                    if n >= 3:
                        dve.wait_ge(s_hghi, b * N + (n - 2))
                        dve.wait_ge(s_hglo, b * N + (n - 2))
                    elif n == 0:
                        dve.wait_ge(s_glo, b + 1)
                    v.tensor_tensor(hg[n % 3], hid[n % 2], bank[2 + e % 2][:, :], ALU.mult).then_inc(s_hg, 1)
                    if n >= 1:
                        m = n - 1
                        dve.wait_ge(s_hghi, b * N + n)
                        if m >= 2:
                            dve.wait_ge(s_dn, b * N + (m - 1))
                        v.tensor_tensor(hg_lo[m % 2][:, :], hg[m % 3], hg_hi[m % 2][:, :].bitcast(fp32),
                                        ALU.subtract).then_inc(s_hglo, 1)
                dve.wait_ge(s_hghi, (b + 1) * N)
                dve.wait_ge(s_dn, (b + 1) * N - 2)
                v.tensor_tensor(hg_lo[1][:, :], hg[(N - 1) % 3], hg_hi[1][:, :].bitcast(fp32), ALU.subtract).then_inc(s_hglo, 1)
                dve.wait_ge(s_yT, b + 1)
                v.tensor_tensor(row(x_all, b), row(x_all, b), bank[6][:, :], ALU.add).then_inc(s_o, 1)

        @block.tensor
        def _(pe):
            t = nc.tensor
            pe.wait_ge(s_const, 16)
            pe.wait_ge(s_small, 80)
            t.transpose(bank[0][:, 0:R_END], small_rows[:, :], ident[0:R_END, 0:R_END]).then_inc(s_colsT, 1)
            pe.wait_ge(s_wqkvo, 80)
            t.transpose(bank[1][:, 0:2 * DH], qk_raw[:, :], ident[:, :])
            t.transpose(bank[2][:, 0:2 * DH], vo_raw[:, :], ident[:, :])
            t.transpose(bank[3][0:DH, 0:D], wout_raw[:, :], ident[:, :]).then_inc(s_wT, 1)
            pe.wait_ge(s_silu, 1)
            pe.wait_ge(s_wmod, 16)
            for m in range(NMOD):
                last = t.matmul(bank[4][:, m * B:(m + 1) * B], wmod_sb[:, m * D:(m + 1) * D], silu_c[:, :], start=True, stop=True)
            last.then_inc(s_mod, 1)
            pe.wait_ge(s_diag, 1)
            for n in range(2):
                last = t.matmul(bank[5 + n][:, :], ones[:, :], diag_ga[:, 4 * n:4 * n + 4, :].rearrange("p b d -> p (b d)"),
                                start=True, stop=True)
            last.then_inc(s_gab, 1)
            pe.wait_ge(s_ready, 3)
            pe.wait_ge(s_bc, 80)

            with pe.Fori(0, PAIRS) as i:
                for p in range(2):
                    pe.wait_ge(s_xn, i * 2 + (p + 1))
                    for j in range(NT):
                        last = t.transpose(bA[p][:, j * P:(j + 1) * P], xn[p][:, j, :], ident[:, :])
                    last.then_inc(s_xT, 1)
                for p in range(2):
                    b = i * 2 + p
                    pe.wait_ge(s_hT, b + 1)
                    t.matmul(bB[p][:, :], wqk[:, :], hT[p][:, :], start=True, stop=True).then_inc(s_qk, 1)
                    pe.wait_ge(s_sq, b + 1)
                    for j in range(NT):
                        last = t.matmul(bA[p][:, j:j + 1], sq[p][:, j * P:(j + 1) * P], mean_col[:, :], start=True, stop=True)
                    last.then_inc(s_ms, 1)
                for p in range(2):
                    for j in range(NT):
                        o = NVO * (j % 2)
                        last = t.matmul((bC, bD)[j // 2][p][:, o:o + NVO], hT[p][:, j * P:(j + 1) * P], wvo[:, :], start=True, stop=True)
                    last.then_inc(s_voz, 1)
                for p in range(2):
                    pe.wait_ge(s_z, i * 2 + (p + 1))
                    F = bA[p][:, 8:8 + NT]
                    t.matmul(F, tri[:, :], zg[p][:, :, 1], start=True, stop=False, skip_group_check=True)
                    for k in range(1, NT):
                        last = t.matmul(F[:, k:NT], ones[:, :], zg[p][:, 0:NT - k, 1], start=False, stop=k == NT - 1, skip_group_check=True)
                    last.then_inc(s_F, 1)
                for p in range(2):
                    pe.wait_ge(s_a, i * 2 + (p + 1))
                    for j in range(NT):
                        last = t.transpose(bA[p][0:1, j * P:(j + 1) * P], a_col[p][:, j:j + 1], ident[:, :])
                    last.then_inc(s_aT, 1)
                for p in range(2):
                    pe.wait_ge(s_qkT, i * 2 + (p + 1))
                    pe.wait_ge(s_v, i * 2 + (p + 1))
                    for j, dst in ((0, bC[p][:, 0:T]), (1, bD[p][:, 0:WIDTH[1]]), (3, bD[p][:, WIDTH[1]:T])):
                        t.matmul(dst, kT[p][:, j * P:(j + 1) * P], qT[p][:, j * P:T], start=True, stop=True).then_inc(s_S, 1)
                    pe.wait_ge(s_M, i * 2 + (p + 1))
                    t.matmul(bB[p][:, :], ones[0:1, :], m_row[p][0:1, :], start=True, stop=True).then_inc(s_Mb, 1)
                    t.matmul(bA[p][:, 0:WIDTH[2]], kT[p][:, 2 * P:3 * P], qT[p][:, 2 * P:T], start=True, stop=True).then_inc(s_S, 1)
                for p in range(2):
                    pe.wait_ge(s_P, (i * 2 + (p + 1)) * NT)
                    for q in range(NT):
                        for j in range(q + 1):
                            o = START[j] + (q - j) * P
                            last = t.matmul(bC[p][:, q * NS:(q + 1) * NS], ew[p][:, o:o + P], vs[p][:, j, :], start=j == 0, stop=j == q)
                    last.then_inc(s_pv, 1)
                for p in range(2):
                    wait_apart(pe, s_hh, i * 2 + (p + 1))
                    for j in range(NT):
                        last = t.transpose(bB[p][0:DH, j * P:(j + 1) * P], hh[p][:, j, :], ident[:, :])
                    last.then_inc(s_hhT, 1)
                for p in range(2):
                    b = i * 2 + p
                    pe.wait_ge(s_hhc, b + 1)
                    dg = diag_ga[:, :, :].rearrange("p b d -> p (b d)")[:, bass.ds(b * D, D)]
                    wg = wout_ga[:, :, :].rearrange("p b d -> p (b d)")[:, bass.ds(b * D, D)]
                    for j in range(NT):
                        dst = bD[p][:, j * P:(j + 1) * P]
                        t.matmul(dst, hT[p][:, j * P:(j + 1) * P], dg, start=True, stop=False)
                        last = t.matmul(dst, hhT[p][:, j * P:(j + 1) * P], wg, start=False, stop=True)
                    last.then_inc(s_x1p, 1)
                for p in range(2):
                    pe.wait_ge(s_xn2, i * 2 + (p + 1))
                    for j in range(NT):
                        last = t.transpose(bA[p][:, j * P:(j + 1) * P], xn[p][:, j, :], ident[:, :])
                    last.then_inc(s_x2T, 1)
                for p in range(2):
                    pe.wait_ge(s_h2hi, i * 2 + (p + 1))
                    for j in range(NT):
                        last = t.matmul(bB[p][:, j * E:(j + 1) * E], h2T[p][:, j * P:(j + 1) * P], wr_sb[:, :], start=True, stop=True)
                    last.then_inc(s_lgp, 1)

            pe.wait_ge(s_gates, 1)
            pe.wait_ge(s_w12, 3)
            pe.wait_ge(s_w, 2)
            pe.wait_ge(s_lo, B)
            with pe.Fori(0, B) as b:
                hx, hl = row(h2_hi, b), row(h2_lo, b)

                def up(n):
                    e, u = divmod(n, NU)
                    if n >= 2:
                        pe.wait_ge(s_hid, b * N + (n - 1))
                    w_hi, w_lo = (w[:, e, u * P:(u + 1) * P] for w in (w1_hi, w1_lo))
                    t.matmul(bank[n % 2][:, :], w_hi, hx, start=True, stop=False)
                    t.matmul(bank[n % 2][:, :], w_hi, hl, start=False, stop=False)
                    t.matmul(bank[n % 2][:, :], w_lo, hx, start=False, stop=True).then_inc(s_up, 1)

                def gate(e):
                    if e >= 2:
                        wait_apart(pe, s_hg, b * N + (e - 1) * NU)
                    t.matmul(bank[2 + e % 2][:, :], sel_r[:, e, :], row(gateT, b), start=True, stop=True).then_inc(s_gb, 1)

                def down(n):
                    e, u = divmod(n, NU)
                    pe.wait_ge(s_hghi, b * N + (n + 1))
                    w_hi, w_lo = w2_hi[:, e, u, :], w2_lo[:, e, u, :]
                    t.matmul(bank[5][:, :], w_hi, hg_hi[n % 2][:, :], start=False, stop=False)
                    t.matmul(bank[5][:, :], w_lo, hg_hi[n % 2][:, :], start=False, stop=False)
                    pe.wait_ge(s_hglo, b * N + (n + 1))
                    t.matmul(bank[5][:, :], w_hi, hg_lo[n % 2][:, :], start=False, stop=n == N - 1).then_inc(s_dn, 1)

                up(0)
                pe.wait_ge(s_gblk, b + 1)
                for k in range(NT):
                    last = t.transpose(bank[7][0:E, k * P:(k + 1) * P], gate_blk[:, k, :], ident[:, :])
                last.then_inc(s_gT, 1)
                up(1)
                wait_apart(pe, s_glo, b + 1)
                gate(0)
                wait_apart(pe, s_ysb, b + 1)
                t.matmul(bank[5][:, :], b2_hi[:, :], row(gateT, b), start=True, stop=False)
                t.matmul(bank[5][:, :], b2_lo[:, :], row(gateT, b), start=False, stop=False)
                gate(1)
                for n in range(2, N):
                    up(n)
                    down(n - 2)
                    if n % NU == 1 and n // NU + 1 < E:
                        gate(n // NU + 1)
                down(N - 2)
                down(N - 1)
                pe.wait_ge(s_ysb, b + 2)
                for k in range(NT):
                    last = t.transpose(bank[6][:, k * P:(k + 1) * P], y_sb[:, k * P:(k + 1) * P], ident[:, :])
                last.then_inc(s_yT, 1)


_INS = ["L0_attn_x", "L0_attn_norm_w", "L0_attn_Wq", "L0_attn_Wk", "L0_attn_Wv", "L0_attn_wi_w", "L0_attn_wi_b",
        "L0_attn_wf_w", "L0_attn_wf_b", "L0_attn_Wo", "L0_attn_bo", "L0_attn_Wout", "L0_ffn_Wr", "L0_ffn_br",
        "L0_ffn_W1", "L0_ffn_b1", "L0_ffn_W2", "L0_ffn_b2", "L0_c", "L0_wmod"]


def kernel(**inputs):
    import numpy as _np
    import concourse.bacc as _bacc
    from concourse import mybir as _mybir
    from concourse.bass_utils import run_bass_kernel_spmd as _run

    nc = _bacc.Bacc("TRN2", target_bir_lowering=False, num_devices=1)
    arrays, args = {}, []
    for name in _INS:
        a = _np.ascontiguousarray(inputs[name])
        arrays[f"in_{name}_dram"] = a
        args.append(nc.dram_tensor(f"in_{name}_dram", a.shape, _mybir.dt.from_np(a.dtype), kind="ExternalInput").ap())
    shape = inputs["L0_attn_x"].shape
    args.append(nc.dram_tensor("out_0_dram", shape, _mybir.dt.float32, kind="ExternalOutput").ap())
    adaln_mlstm_moe_kernel(nc, *args)
    r = _run(nc, [arrays], core_ids=[0])
    return r.results[0]["out_0_dram"]
```

```python
import concourse.bass as bass
from concourse import mybir
from contextlib import ExitStack


def adaln_mlstm_moe_kernel(
    nc: bass.Bass,
    x_in: bass.AP,
    norm_w: bass.AP,
    Wq: bass.AP,
    Wk: bass.AP,
    Wv: bass.AP,
    wi_w: bass.AP,
    wi_b: bass.AP,
    wf_w: bass.AP,
    wf_b: bass.AP,
    Wo: bass.AP,
    bo: bass.AP,
    Wout: bass.AP,
    Wr: bass.AP,
    br: bass.AP,
    W1: bass.AP,
    b1: bass.AP,
    W2: bass.AP,
    b2: bass.AP,
    c_in: bass.AP,
    wmod: bass.AP,
    out: bass.AP,
):
    fp32 = mybir.dt.float32
    fp32r = mybir.dt.float32r
    u32 = mybir.dt.uint32
    ALU = mybir.AluOpType
    ACT = mybir.ActivationFunctionType

    P = 128
    B, T, D = x_in.shape
    DH = Wq.shape[0]
    E = Wr.shape[1]
    FF = W1.shape[2]
    NT = T // P
    NU = FF // P
    N = E * NU
    LAG = 3
    NMOD = wmod.shape[1] // D
    LN_EPS, RMS_EPS = 1e-5, 1e-6
    SCALE = float(DH) ** -0.5
    FAR = 1e30
    NZ = DH + 2
    NS = DH + 1
    LO = 32
    GK = LO + E
    R_C, R_B1, R_WI, R_WF, R_NORM, R_END = 0, B, B + E * NU, B + E * NU + 1, B + E * NU + 2, B + E * NU + 3
    WIDTH = [T - P * j for j in range(NT)]
    START = [sum(WIDTH[:j]) for j in range(NT)]
    NW = sum(WIDTH)
    CONSTS = 8 + E
    POOL_STEPS = (1, 8, 9, 10, 11, 12, 13, 14, 15)

    ctx = ExitStack()
    with ctx:
        def sb(name, shape, dt=fp32):
            return ctx.enter_context(nc.sbuf_tensor(name, shape, dt))

        def sem(name):
            return ctx.enter_context(nc.semaphore(name))

        ident = sb("ident", [P, P])
        ones = sb("ones", [P, P])
        tri = sb("tri", [P, P])
        far = sb("far", [P, P])
        mean_col = sb("mean_col", [P, 1])
        neg_row = sb("neg_row", [1, T])
        iota_e = sb("iota_e", [P, E])
        minus_half = sb("minus_half", [P, NT])
        sel_r = sb("sel_r", [GK, E, P], fp32r)
        small_rows = sb("small_rows", [R_END, D])
        qk_raw = sb("qk_raw", [2 * DH, D])
        vo_raw = sb("vo_raw", [2 * DH, D])
        wout_raw = sb("wout_raw", [D, DH])
        wmod_sb = sb("wmod_sb", [D, NMOD * D])
        w1_raw = sb("w1_raw", [D, E, FF])
        w2_raw = sb("w2_raw", [P, E, NU, D])
        b2_raw = sb("b2_raw", [GK, D])
        wr_sb = sb("wr_sb", [D, E])
        zb_bc = sb("zb_bc", [P, 2])
        bo_bc = sb("bo_bc", [P, DH])
        br_bc = sb("br_bc", [P, E])
        cols = sb("cols", [P, R_END])
        silu_c = sb("silu_c", [P, B])
        tanh_c = sb("tanh_c", [P, B])
        mods = sb("mods", [P, NMOD, B])
        sign_g = sb("sign_g", [P, 2, B])
        mag_g = sb("mag_g", [P, 2, B])
        wqk = sb("wqk", [D, 2 * DH])
        wvz = sb("wvz", [D, NZ])
        wo = sb("wo", [D, DH])
        woutT = sb("woutT", [DH, D])
        diag_ga = sb("diag_ga", [P, B, D])
        wout_ga = sb("wout_ga", [DH, B, D])
        w1_hi = sb("w1_hi", [D, E, FF], fp32r)
        w1_lo = sb("w1_lo", [D, E, FF], fp32r)
        w2_hi = sb("w2_hi", [P, E, NU, D], fp32r)
        w2_lo = sb("w2_lo", [P, E, NU, D], fp32r)
        b2_hi = sb("b2_hi", [GK, D], fp32r)
        b2_lo = sb("b2_lo", [GK, D], fp32r)
        x_all = sb("x_all", [P, B * T])
        h2_hi = sb("h2_hi", [D, B * T], fp32r)
        h2_lo = sb("h2_lo", [D, B * T], fp32r)
        gateT = sb("gateT", [GK, B * T], fp32r)
        stats = [sb(f"stats{k}", [P, NT, 6]) for k in range(2)]
        mv = [sb(f"mv{k}", [P, NT, 2]) for k in range(2)]
        var_eps = [sb(f"var_eps{k}", [P, NT]) for k in range(2)]
        rstd = [sb(f"rstd{k}", [P, NT]) for k in range(2)]
        xn = [sb(f"xn{k}", [P, NT, D]) for k in range(2)]
        xc = [sb(f"xc{k}", [P, NT, D]) for k in range(2)]
        hT = sb("hT", [D, T])
        sq = sb("sq", [D, T])
        ms_eps = sb("ms_eps", [P, NT])
        rms = sb("rms", [P, NT])
        rms2 = sb("rms2", [P, NT])
        rms_inv = sb("rms_inv", [P, NT])
        qT = sb("qT", [DH, T])
        kT = sb("kT", [DH, T])
        zg = sb("zg", [P, NT, 2])
        zp = sb("zp", [P, NT - 1])
        vs = sb("vs", [P, NT, NS])
        zo = sb("zo", [P, NT, DH])
        th = sb("th", [P, NT, DH])
        a_col = sb("a_col", [P, NT])
        m_row = sb("m_row", [1, T])
        mb = sb("mb", [P, NT, P])
        ew = sb("ew", [P, NW])
        den = sb("den", [P, NT])
        rden = sb("rden", [P, NT])
        uh = sb("uh", [P, NT, DH])
        hh = sb("hh", [P, NT, DH])
        hhT = sb("hhT", [DH, T])
        h2T = sb("h2T", [D, T])
        lg = sb("lg", [P, NT, E])
        mx = sb("mx", [P, NT, 8])
        ix = sb("ix", [P, NT, 8], u32)
        top_d = sb("top_d", [P, NT])
        top_e2 = sb("top_e2", [P, NT])
        top_s = sb("top_s", [P, NT])
        top_g = sb("top_g", [P, 2, NT])
        gate_a = sb("gate_a", [P, NT, E])
        gate_b = sb("gate_b", [P, NT, E])
        gates = sb("gates", [P, NT, E])
        hid = [sb(f"hid{k}", [P, T]) for k in range(4)]
        hg = [sb(f"hg{k}", [P, T]) for k in range(4)]
        hg_hi = [sb(f"hg_hi{k}", [P, T], fp32r) for k in range(4)]
        hg_lo = [sb(f"hg_lo{k}", [P, T], fp32r) for k in range(4)]
        y_sb = sb("y_sb", [D, T])
        sel = ew[0:GK, 0:E * P].rearrange("k (e m) -> k e m", e=E)

        bank = [ctx.enter_context(nc.psum_tensor(f"bank{k}", [P, 512], fp32)) for k in range(8)]
        up_bank, gate_bank, y_bank = bank[0:2], bank[2:4], bank[4]
        bA, bB, bC = bank[5], bank[6], bank[7]

        s_small = sem("s_small")
        s_wqkvo = sem("s_wqkvo")
        s_wmod = sem("s_wmod")
        s_bc = sem("s_bc")
        s_w1 = sem("s_w1")
        s_w2 = sem("s_w2")
        s_b2 = sem("s_b2")
        s_x0 = sem("s_x0")
        s_x_row1 = sem("s_x_row1")
        s_x_rest = sem("s_x_rest")
        s_const = sem("s_const")
        s_pool = sem("s_pool")
        s_colsT = sem("s_colsT")
        s_wT = sem("s_wT")
        s_cols = sem("s_cols")
        s_tanhc = sem("s_tanhc")
        s_silu = sem("s_silu")
        s_mod = sem("s_mod")
        s_proj = sem("s_proj")
        s_dve0 = sem("s_dve0")
        s_mods = sem("s_mods")
        s_diag = sem("s_diag")
        s_gab = sem("s_gab")
        s_wga = sem("s_wga")
        s_sel = sem("s_sel")
        s_b2z = sem("s_b2z")
        s_b2h = sem("s_b2h")
        s_b2l = sem("s_b2l")
        s_whi = sem("s_whi")
        s_wlo = sem("s_wlo")
        s_st = [sem(f"s_st{k}") for k in range(2)]
        s_mv = [sem(f"s_mv{k}") for k in range(2)]
        s_ve = [sem(f"s_ve{k}") for k in range(2)]
        s_rs = [sem(f"s_rs{k}") for k in range(2)]
        s_xc = [sem(f"s_xc{k}") for k in range(2)]
        s_xn = [sem(f"s_xn{k}") for k in range(2)]
        s_xT = sem("s_xT")
        s_hT = sem("s_hT")
        s_sq = sem("s_sq")
        s_qk = sem("s_qk")
        s_qkT = sem("s_qkT")
        s_ms = sem("s_ms")
        s_mse = sem("s_mse")
        s_rms = sem("s_rms")
        s_rms2 = sem("s_rms2")
        s_ob = sem("s_ob")
        s_vz = sem("s_vz")
        s_z = sem("s_z")
        s_zp = sem("s_zp")
        s_v = sem("s_v")
        s_zo = sem("s_zo")
        s_th = sem("s_th")
        s_F = sem("s_F")
        s_a = sem("s_a")
        s_aT = sem("s_aT")
        s_M = sem("s_M")
        s_Mb = sem("s_Mb")
        s_mask = sem("s_mask")
        s_E = sem("s_E")
        s_S = sem("s_S")
        s_P = sem("s_P")
        s_pv = sem("s_pv")
        s_den = sem("s_den")
        s_rd = sem("s_rd")
        s_hh = sem("s_hh")
        s_hhT = sem("s_hhT")
        s_hhc = sem("s_hhc")
        s_x1p = sem("s_x1p")
        s_x1 = sem("s_x1")
        s_x2T = sem("s_x2T")
        s_h2 = sem("s_h2")
        s_h2hi = sem("s_h2hi")
        s_h2lo = sem("s_h2lo")
        s_lgp = sem("s_lgp")
        s_lg = sem("s_lg")
        s_mx = sem("s_mx")
        s_ix = sem("s_ix")
        s_td = sem("s_td")
        s_te = sem("s_te")
        s_ts = sem("s_ts")
        s_g1 = sem("s_g1")
        s_g2 = sem("s_g2")
        s_gab2 = sem("s_gab2")
        s_gates = sem("s_gates")
        s_gT = sem("s_gT")
        s_ghi = sem("s_ghi")
        s_glo = sem("s_glo")
        s_gb = sem("s_gb")
        s_up = sem("s_up")
        s_hid = sem("s_hid")
        s_hg = sem("s_hg")
        s_hghi = sem("s_hghi")
        s_lo_dve = sem("s_lo_dve")
        s_lo_pool = sem("s_lo_pool")
        s_dn = sem("s_dn")
        s_ysb = sem("s_ysb")
        s_yT = sem("s_yT")
        s_o = sem("s_o")
        s_out = sem("s_out")

        block = ctx.enter_context(nc.Block())

        x_v = x_in.rearrange("b (j p) d -> b p j d", p=P)
        out_v = out.rearrange("b (j p) d -> b p j d", p=P)

        def row(ap, b):
            return ap[:, bass.ds(b * T, T)]

        def bcast(ap, n):
            return ap.unsqueeze(2).to_broadcast([ap.shape[0], ap.shape[1], n])

        def wait_apart(eng, of, value):
            value = eng.to_reg(value)
            eng.wait_ge(s_const, CONSTS)
            eng.wait_ge(of, value)

        def los(n, by_pool):
            return sum(1 for m in range(n + 1) if (m % N in POOL_STEPS) == by_pool)

        def last_turns(body):
            body(B - 3, True, True, False, lambda n: True)
            body(B - 2, True, False, False, lambda n: True)
            body(B - 1, False, False, False, lambda n: n < N)

        @block.sync
        def _(sp):
            def load_x(b, n, of):
                sp.dma_start(x_all[:, b * T:(b + n) * T].rearrange("p (j d) -> p j d", j=n * NT),
                             x_v[b:b + n].rearrange("b p j d -> p b j d").rearrange("p b j d -> p (b j) d")).then_inc(of, 16)

            sp.dma_start(small_rows[R_C:R_C + B, :], c_in).then_inc(s_small, 16)
            sp.dma_start(small_rows[R_B1:R_WI, :], b1.rearrange("e (u f) -> (e u) f", f=P)).then_inc(s_small, 16)
            sp.dma_start(small_rows[R_WI:R_WF, :], wi_w).then_inc(s_small, 16)
            load_x(0, 1, s_x0)
            sp.dma_start(wmod_sb[:, :], wmod).then_inc(s_wmod, 16)
            load_x(1, 1, s_x_row1)
            sp.dma_start(wr_sb[:, :], Wr).then_inc(s_bc, 16)
            sp.dma_start(zb_bc[:, 0:1], wi_b.partition_broadcast(P)).then_inc(s_bc, 16)
            sp.dma_start(zb_bc[:, 1:2], wf_b.partition_broadcast(P)).then_inc(s_bc, 16)
            sp.dma_start(bo_bc[:, :], bo.partition_broadcast(P)).then_inc(s_bc, 16)
            sp.dma_start(br_bc[:, :], br.partition_broadcast(P)).then_inc(s_bc, 16)
            sp.dma_start(w1_raw[:, :, :], W1.rearrange("e h f -> h e f")).then_inc(s_w1, 16)
            sp.dma_start(w2_raw[:, :, :, :].rearrange("f e u h -> f (e u) h"),
                         W2.rearrange("e (u f) h -> f (e u) h", f=P)).then_inc(s_w2, 16)
            sp.dma_start(b2_raw[0:E, :], b2).then_inc(s_b2, 16)
            sp.dma_start(b2_raw[LO:LO + E, :], b2).then_inc(s_b2, 16)
            load_x(2, B - 2, s_x_rest)
            with sp.Fori(0, B) as b:
                sp.wait_ge(s_o, b + 1)
                sp.dma_start(out_v[bass.ds(b, 1)].rearrange("b p j d -> p (b j) d"),
                             row(x_all, b).rearrange("p (j d) -> p j d", j=NT)).then_inc(s_out, 16)
            sp.wait_ge(s_out, 16 * B)

        @block.gpsimd
        def _(pool):
            g = nc.gpsimd
            g.memset(ident[:, :], 0.0).then_inc(s_pool, 1)
            g.memset(tri[:, :], 1.0).then_inc(s_pool, 1)
            g.memset(far[:, :], 0.0).then_inc(s_pool, 1)
            g.memset(sel, 0.0).then_inc(s_pool, 1)
            g.memset(minus_half[:, :], -0.5).then_inc(s_const, 1)
            pool.wait_ge(s_pool, 4)
            g.affine_select(out=ident[:, :], in_=ident[:, :], compare_op=ALU.not_equal, fill=1.0, base=0,
                            pattern=[[-1, P]], channel_multiplier=1).then_inc(s_const, 1)
            g.memset(ones[:, :], 1.0).then_inc(s_const, 1)
            g.memset(mean_col[:, :], 1.0 / D).then_inc(s_const, 1)
            g.memset(neg_row[:, :], -3e38).then_inc(s_const, 1)
            for e in range(E):
                g.memset(iota_e[:, e:e + 1], float(e)).then_inc(s_const, 1)
            g.affine_select(out=tri[:, :], in_=tri[:, :], compare_op=ALU.is_ge, fill=0.0, base=0,
                            pattern=[[1, P]], channel_multiplier=-1).then_inc(s_const, 1)
            g.affine_select(out=far[:, :], in_=far[:, :], compare_op=ALU.is_ge, fill=FAR, base=0,
                            pattern=[[1, P]], channel_multiplier=-1).then_inc(s_const, 1)
            g.affine_select(out=sel, in_=sel, compare_op=ALU.not_equal, fill=1.0, base=0,
                            pattern=[[-1, E], [0, P]], channel_multiplier=1).then_inc(s_pool, 1)
            pool.wait_ge(s_pool, 5)
            g.affine_select(out=sel, in_=sel, compare_op=ALU.not_equal, fill=1.0, base=-LO,
                            pattern=[[-1, E], [0, P]], channel_multiplier=1).then_inc(s_const, 1)
            pool.wait_ge(s_const, CONSTS)

            def norm(k, b, first=False):
                wait_apart(pool, s_mv[k], b + 1)
                g.tensor_scalar(var_eps[k][:, :], mv[k][:, :, 1], LN_EPS, None, ALU.add).then_inc(s_ve[k], 1)
                g.tensor_tensor(xc[k][:, :, :], row(x_all, b).rearrange("p (j d) -> p j d", j=NT), 
                                bcast(mv[k][:, :, 0], D), ALU.subtract).then_inc(s_xc[k], 1)
                pool.wait_ge(s_ve[k], b + 1)
                g.tensor_tensor(rstd[k][:, :], var_eps[k][:, :], minus_half[:, :], ALU.pow).then_inc(s_rs[k], 1)
                pool.wait_ge(s_xc[k], b + 1)
                if k == 0 and not first:
                    wait_apart(pool, s_xT, b)
                wait_apart(pool, s_rs[k], b + 1)
                g.tensor_tensor(xn[k][:, :, :], xc[k][:, :, :], bcast(rstd[k][:, :], D), ALU.mult).then_inc(s_xn[k], 1)

            def body(b, end, start, ahead, live):
                m1, m2 = b + 1, b + 2
                for t in range(LAG, N + LAG):
                    if t == 7 and end:
                        norm(1, m1)
                    if t == 8 and start:
                        pool.wait_ge(s_mse, m2 + 1)
                        g.tensor_tensor(rms[:, :], ms_eps[:, :], minus_half[:, :], ALU.pow).then_inc(s_rms, 1)
                    if t == 5 and ahead:
                        norm(0, b + 3)
                    if t == 10 and end:
                        pool.wait_ge(s_h2, m1 + 1)
                        pool.wait_ge(s_h2hi, m1 + 1)
                        g.tensor_tensor(row(h2_lo, m1), h2T[:, :], row(h2_hi, m1).bitcast(fp32), ALU.subtract).then_inc(s_h2lo, 1)
                    if live(t - 1) and (t - 1) % N in POOL_STEPS:
                        k = (t - 1) % 4
                        pool.wait_ge(s_hghi, b * N + t)
                        g.tensor_tensor(hg_lo[k][:, :], hg[k][:, :], hg_hi[k][:, :].bitcast(fp32), ALU.subtract).then_inc(s_lo_pool, 1)

            norm(0, 0, first=True)
            body(-2, False, True, True, lambda n: False)
            g.memset(gateT[:, :].bitcast(fp32), 0.0).then_inc(s_sel, 1)
            pool.wait_ge(s_whi, 1)
            g.tensor_tensor(w1_lo[:, :, :], w1_raw[:, :, :], w1_hi[:, :, :].bitcast(fp32), ALU.subtract).then_inc(s_wlo, 1)
            pool.wait_ge(s_whi, 2)
            g.tensor_tensor(w2_lo[:, :, :, :], w2_raw[:, :, :, :], w2_hi[:, :, :, :].bitcast(fp32), ALU.subtract).then_inc(s_wlo, 1)
            body(-1, True, True, True, lambda n: n >= N)
            with pool.Fori(0, B - 3) as b:
                body(b, True, True, True, lambda n: True)
            last_turns(body)

        @block.scalar
        def _(act):
            a = nc.scalar
            act.dma_start(small_rows[R_WF:R_NORM, :], wf_w).then_inc(s_small, 16)
            act.dma_start(small_rows[R_NORM:R_END, :], norm_w.rearrange("(a n) -> a n", a=1)).then_inc(s_small, 16)
            act.dma_start(qk_raw[0:DH, :], Wq).then_inc(s_wqkvo, 16)
            act.dma_start(qk_raw[DH:2 * DH, :], Wk).then_inc(s_wqkvo, 16)
            act.dma_start(vo_raw[0:DH, :], Wv).then_inc(s_wqkvo, 16)
            act.dma_start(vo_raw[DH:2 * DH, :], Wo).then_inc(s_wqkvo, 16)
            act.dma_start(wout_raw[:, :], Wout).then_inc(s_wqkvo, 16)
            act.wait_ge(s_cols, 1)
            a.activation(tanh_c[:, :], cols[:, R_C:R_C + B], ACT.Tanh, scale=0.5).then_inc(s_tanhc, 1)
            act.wait_ge(s_mods, 1)

            def weights(p, j):
                last = a.activation(ew[:, START[j]:START[j] + P], mb[:, j, :], ACT.Exp, bias=a_col[:, j:j + 1], scale=-1.0)
                if j < NT - 1:
                    last = a.activation(ew[:, START[j] + P:START[j] + WIDTH[j]], bB[:, P * (j + 1):T],
                                        ACT.Exp, bias=a_col[:, j:j + 1], scale=-1.0)
                last.then_inc(s_E, 1)

            def body(b, end, start, ahead, live, weights_hi=False):
                m1, m2 = b + 1, b + 2
                for t in range(LAG, N + LAG):
                    if live(t):
                        n = t % N
                        act.wait_ge(s_up, b * N + (t + 1))
                        a.activation(hid[n % 4][:, :], up_bank[n % 2][:, :], ACT.Relu,
                                     bias=cols[:, R_B1 + n:R_B1 + n + 1]).then_inc(s_hid, 1)
                    if t == N - 1 and end:
                        act.wait_ge(s_gT, m1 + 1)
                        a.activation(row(gateT, m1)[0:E, :], gate_bank[0][0:E, :], ACT.Copy).then_inc(s_ghi, 1)
                    if live(t - 1):
                        k = (t - 1) % 4
                        act.wait_ge(s_hg, b * N + t)
                        a.activation(hg_hi[k][:, :], hg[k][:, :], ACT.Copy).then_inc(s_hghi, 1)
                    if t == 4 and end:
                        act.wait_ge(s_hhT, m1 + 1)
                        a.activation(hhT[:, :], bB[0:DH, :], ACT.Copy).then_inc(s_hhc, 1)
                    if t == 5 and start:
                        act.wait_ge(s_xT, m2 + 1)
                        a.activation(hT[:, :], bA[:, :], ACT.Identity, bias=mods[:, 0, bass.ds(m2, 1)],
                                     scale=mods[:, 1, bass.ds(m2, 1)]).then_inc(s_hT, 1)
                    if t == 6 and start:
                        a.activation(sq[:, :], bA[:, :], ACT.Square, bias=mods[:, 0, bass.ds(m2, 1)],
                                     scale=mods[:, 1, bass.ds(m2, 1)]).then_inc(s_sq, 1)
                    if t == 7 and start:
                        act.wait_ge(s_qk, m2 + 1)
                        a.activation(qT[:, :], bB[0:DH, :], ACT.Copy)
                        a.activation(kT[:, :], bB[DH:2 * DH, :], ACT.Copy).then_inc(s_qkT, 1)
                        if weights_hi:
                            act.wait_ge(s_w1, 16)
                            a.activation(w1_hi[:, :, :], w1_raw[:, :, :], ACT.Copy).then_inc(s_whi, 1)
                            act.wait_ge(s_w2, 16)
                            a.activation(w2_hi[:, :, :, :], w2_raw[:, :, :, :], ACT.Copy).then_inc(s_whi, 1)
                    if t == 9 and end:
                        act.wait_ge(s_x2T, m1 + 1)
                        sh, sc = mods[:, 3, bass.ds(m1, 1)], mods[:, 4, bass.ds(m1, 1)]
                        a.activation(h2T[:, :], bC[:, :], ACT.Identity, bias=sh, scale=sc).then_inc(s_h2, 1)
                        a.activation(row(h2_hi, m1), bC[:, :], ACT.Identity, bias=sh, scale=sc).then_inc(s_h2hi, 1)
                    if t == 10 and start:
                        act.wait_ge(s_zo, m2 + 1)
                        a.activation(th[:, :, :], zo[:, :, :], ACT.Tanh, scale=0.5).then_inc(s_th, 1)
                    if t == 12 and end:
                        act.wait_ge(s_td, m1 + 1)
                        a.activation(top_e2[:, :], top_d[:, :], ACT.Exp).then_inc(s_te, 1)
                    if start and t in (14, 15, 16):
                        if t == 14:
                            act.wait_ge(s_mask, m2 + 1)
                        if t == 16:
                            weights(m2, 3)
                        weights(m2, t - 14)
                if live(N - 1):
                    act.wait_ge(s_dn, b * N + N)
                    a.activation(y_sb[:, :], y_bank[:, :], ACT.Copy, scale=mods[:, 5, bass.ds(b, 1)]).then_inc(s_ysb, 1)

            body(-2, False, True, True, lambda n: False, weights_hi=True)
            body(-1, True, True, True, lambda n: n >= N)
            with act.Fori(0, B - 3) as b:
                body(b, True, True, True, lambda n: True)
            last_turns(body)

        @block.vector
        def _(dve):
            v = nc.vector

            def norm_stats(k, b):
                for j in range(NT):
                    last = v.bn_stats(stats[k][:, j, :], x_all[:, bass.ds(b * T + j * P, P)])
                last.then_inc(s_st[k], 1)

            def norm_aggr(k, b):
                wait_apart(dve, s_st[k], b + 1)
                for j in range(NT):
                    last = v.bn_aggr(mv[k][:, j, :], stats[k][:, j, :])
                last.then_inc(s_mv[k], 1)

            dve.wait_ge(s_colsT, 1)
            v.tensor_copy(cols[:, :], bank[0][:, 0:R_END]).then_inc(s_cols, 1)
            dve.wait_ge(s_tanhc, 1)
            v.scalar_tensor_tensor(silu_c[:, :], tanh_c[:, :], 1.0, cols[:, R_C:R_C + B], ALU.add, ALU.mult).then_inc(s_silu, 1)
            dve.wait_ge(s_x0, 16)
            norm_stats(0, 0)
            norm_aggr(0, 0)
            dve.wait_ge(s_wT, 1)
            nw = cols[:, R_NORM:R_NORM + 1]
            v.tensor_scalar(wqk[:, :], bank[1][:, 0:2 * DH], nw, SCALE, ALU.mult, ALU.mult)
            v.tensor_scalar(wvz[:, 0:DH], bank[2][:, 0:DH], nw, None, ALU.mult)
            v.tensor_scalar(wvz[:, DH:NZ], cols[:, R_WI:R_WF + 1], nw, None, ALU.mult)
            v.tensor_scalar(wo[:, :], bank[2][:, DH:2 * DH], nw, None, ALU.mult)
            v.tensor_copy(woutT[:, :], bank[3][0:DH, 0:D]).then_inc(s_proj, 1)
            dve.wait_ge(s_mod, 1)
            md = bank[4][:, 0:NMOD * B].rearrange("p (m b) -> p m b", m=NMOD)
            for m in (3, 0):
                v.tensor_scalar(mods[:, m, :], md[:, m, :], 0.5, None, ALU.mult)
                last = v.tensor_scalar(mods[:, m + 1, :], md[:, m + 1, :], 0.5, 1.0, ALU.mult, ALU.add)
            last.then_inc(s_mods, 1)
            for n, m in enumerate((2, 5)):
                v.tensor_scalar(sign_g[:, n, :], md[:, m, :], 0.0, 1.0, ALU.is_ge, ALU.mult)
                v.tensor_scalar(mods[:, m, :], md[:, m, :], 0.5, 0.25, ALU.mult, ALU.max)
                last = v.tensor_scalar(mag_g[:, n, :], md[:, m, :], -0.5, 0.25, ALU.mult, ALU.max)
            last.then_inc(s_dve0, 1)
            dve.wait_ge(s_dve0, 1)
            v.tensor_scalar(sign_g[:, :, :], sign_g[:, :, :], 2.0, -1.0, ALU.mult, ALU.add)
            v.tensor_tensor(mag_g[:, 0, :], mag_g[:, 0, :], mods[:, 2, :], ALU.max)
            v.tensor_tensor(mag_g[:, 1, :], mag_g[:, 1, :], mods[:, 5, :], ALU.max).then_inc(s_dve0, 1)
            dve.wait_ge(s_dve0, 2)
            v.tensor_tensor(mods[:, 2, :], sign_g[:, 0, :], mag_g[:, 0, :], ALU.mult)
            v.tensor_tensor(mods[:, 5, :], sign_g[:, 1, :], mag_g[:, 1, :], ALU.mult).then_inc(s_dve0, 1)
            dve.wait_ge(s_const, CONSTS)
            v.tensor_copy(sel_r[:, :, :], sel).then_inc(s_sel, 1)

            def row_diag():
                dve.wait_ge(s_dve0, 3)
                v.tensor_tensor(diag_ga[:, :, :], ident[:, :].unsqueeze(1).to_broadcast([P, B, D]),
                                bcast(mods[:, 2, :], D), ALU.mult).then_inc(s_diag, 1)

            def row_weights():
                dve.wait_ge(s_gab, 1)
                for n in range(2):
                    v.scalar_tensor_tensor(wout_ga[:, 4 * n:4 * n + 4, :],
                                           bank[n][0:DH, :].rearrange("p (b d) -> p b d", b=4), 0.5,
                                           woutT[:, :].unsqueeze(1).to_broadcast([DH, 4, D]),
                                           ALU.mult, ALU.mult).then_inc(s_wga, 1)

            def b2_parts():
                v.memset(b2_hi[:, :].bitcast(fp32), 0.0)
                v.memset(b2_lo[:, :].bitcast(fp32), 0.0).then_inc(s_b2z, 1)
                dve.wait_ge(s_b2z, 1)
                dve.wait_ge(s_b2, 32)
                v.tensor_copy(b2_hi[0:E, :], b2_raw[0:E, :])
                v.tensor_copy(b2_hi[LO:LO + E, :], b2_raw[LO:LO + E, :]).then_inc(s_b2h, 1)
                dve.wait_ge(s_b2h, 1)
                v.tensor_tensor(b2_lo[0:E, :], b2_raw[0:E, :], b2_hi[0:E, :].bitcast(fp32), ALU.subtract).then_inc(s_b2l, 1)

            def scores_times_weights(m, j):
                src = (bC[:, 0:T], bA[:, 0:WIDTH[1]], bC[:, 0:WIDTH[2]], bA[:, WIDTH[1]:T])[j]
                dve.wait_ge(s_E, m * NT + (1, 2, 4, 3)[j])
                dve.wait_ge(s_S, m * NT + (1, 3, 4, 3)[j])
                w = ew[:, START[j]:START[j] + WIDTH[j]]
                v.tensor_tensor(w, w, src, ALU.mult).then_inc(s_P, 1)

            def body(b, end, start, ahead, live, first=False):
                m1, m2 = b + 1, b + 2

                def middle(t):
                    if end:
                        if t == 3:
                            dve.wait_ge(s_den, m1 * 2 + 2)
                            v.reciprocal(rden[:, :], den[:, :]).then_inc(s_rd, 1)
                        if t == 6:
                            wait_apart(dve, s_x1, m1 + 1)
                            norm_stats(1, m1)
                        if t == 11:
                            dve.wait_ge(s_lgp, m1 + 1)
                            v.tensor_tensor(lg[:, :, :], bC[:, 0:NT * E].rearrange("p (j e) -> p j e", j=NT),
                                            br_bc[:, :].unsqueeze(1).to_broadcast([P, NT, E]), ALU.add).then_inc(s_lg, 1)
                        if t == 12:
                            dve.wait_ge(s_mx, m1 + 1)
                            v.tensor_tensor(top_d[:, :], mx[:, :, 1], mx[:, :, 0], ALU.subtract).then_inc(s_td, 1)
                            for j in range(NT):
                                last = v.max_index(ix[:, j, :], mx[:, j, :], lg[:, j, :])
                            last.then_inc(s_ix, 1)
                        if t == 13:
                            dve.wait_ge(s_te, m1 + 1)
                            v.tensor_scalar(top_s[:, :], top_e2[:, :], 1.0, None, ALU.add).then_inc(s_ts, 1)
                            dve.wait_ge(s_ix, m1 + 1)
                            v.tensor_tensor(gate_a[:, :, :], iota_b, ix[:, :, 0:1].to_broadcast([P, NT, E]), ALU.is_equal)
                            v.tensor_tensor(gate_b[:, :, :], iota_b, ix[:, :, 1:2].to_broadcast([P, NT, E]), ALU.is_equal)
                        if t == 14:
                            dve.wait_ge(s_g1, m1 + 1)
                            v.tensor_tensor(top_g[:, 1, :], top_g[:, 0, :], top_e2[:, :], ALU.mult).then_inc(s_g2, 1)
                            v.tensor_tensor(gate_a[:, :, :], gate_a[:, :, :], bcast(top_g[:, 0, :], E), ALU.mult)
                    if start:
                        if t == 9:
                            dve.wait_ge(s_rms, m2 + 1)
                            v.tensor_tensor(rms2[:, :], rms[:, :], rms[:, :], ALU.mult).then_inc(s_rms2, 1)
                            v.reciprocal(rms_inv[:, :], rms[:, :])
                            v.tensor_copy(vs[:, :, DH], rms[:, :])
                        if t == 10:
                            dve.wait_ge(s_vz, m2 + 1)
                            for j in range(NT):
                                last = v.scalar_tensor_tensor(zg[:, j, :], vz[:, j, DH:NZ], rms[:, j:j + 1],
                                                              zb_bc[:, :], ALU.mult, ALU.add)
                            last.then_inc(s_z, 1)
                            wait_apart(dve, s_z, m2 + 1)
                            v.tensor_tensor_scan(zp[:, :], ones[:, 0:NT - 1], zg[:, 0:NT - 1, 1], 0.0, ALU.mult, ALU.add).then_inc(s_zp, 1)
                        if t in (15, 17):
                            scores_times_weights(m2, t - 15)
                    if ahead and t == 4:
                        norm_stats(0, b + 3)

                def after(t):
                    if end:
                        if t == 3:
                            dve.wait_ge(s_rd, m1 + 1)
                            v.tensor_tensor(hh[:, :, :], uh[:, :, :], bcast(rden[:, :], DH), ALU.mult).then_inc(s_hh, 1)
                        if t == 5:
                            dve.wait_ge(s_x1p, m1 + 1)
                            v.tensor_tensor(row(x_all, m1), row(x_all, m1), bC[:, :], ALU.add).then_inc(s_x1, 1)
                        if t == 6:
                            norm_aggr(1, m1)
                        if t == 11:
                            wait_apart(dve, s_lg, m1 + 1)
                            for j in range(NT):
                                last = v.max(mx[:, j, :], lg[:, j, :])
                            last.then_inc(s_mx, 1)
                        if t == 13:
                            dve.wait_ge(s_ts, m1 + 1)
                            v.reciprocal(top_g[:, 0, :], top_s[:, :]).then_inc(s_g1, 1)
                        if t == 14:
                            dve.wait_ge(s_g2, m1 + 1)
                            v.tensor_tensor(gate_b[:, :, :], gate_b[:, :, :], bcast(top_g[:, 1, :], E), ALU.mult).then_inc(s_gab2, 1)
                    if start:
                        if t == 7:
                            dve.wait_ge(s_ms, m2 + 1)
                            v.tensor_scalar(ms_eps[:, :], bA[:, 0:NT], RMS_EPS, None, ALU.add).then_inc(s_mse, 1)
                        if t == 9:
                            dve.wait_ge(s_ob, m2 + 1)
                            for j in range(NT):
                                last = v.scalar_tensor_tensor(zo[:, j, :], bB[:, j * DH:(j + 1) * DH], rms[:, j:j + 1],
                                                              bo_bc[:, :], ALU.mult, ALU.add)
                            last.then_inc(s_zo, 1)
                        if t == 10:
                            dve.wait_ge(s_rms2, m2 + 1)
                            v.tensor_tensor(vs[:, :, 0:DH], vz[:, :, 0:DH], bcast(rms2[:, :], DH), ALU.mult).then_inc(s_v, 1)
                        if t == 11:
                            dve.wait_ge(s_F, m2 + 1)
                            v.tensor_tensor(a_col[:, :], zg[:, :, 0], bA[:, F0:F0 + NT], ALU.subtract).then_inc(s_a, 1)
                        if t == 12:
                            dve.wait_ge(s_aT, m2 + 1)
                            v.tensor_tensor_scan(m_row[0:1, :], bA[0:1, :], neg_row[0:1, :], -3e38, ALU.max, ALU.max).then_inc(s_M, 1)
                        if t == 13:
                            dve.wait_ge(s_Mb, m2 + 1)
                            v.tensor_tensor(mb[:, :, :], bB[:, :].rearrange("p (j t) -> p j t", j=NT),
                                            far[:, :].unsqueeze(1).to_broadcast([P, NT, P]), ALU.add).then_inc(s_mask, 1)
                        if t == 15:
                            scores_times_weights(m2, 1)
                        if t == 16:
                            scores_times_weights(m2, 3)
                    if end and t == 14:
                        dve.wait_ge(s_gab2, m1 + 1)
                        v.tensor_tensor(gates[:, :, :], gate_a[:, :, :], gate_b[:, :, :], ALU.add).then_inc(s_gates, 1)
                    if ahead and t == 4:
                        if first:
                            dve.wait_ge(s_xn[0], 1)
                        norm_aggr(0, b + 3)

                for t in range(LAG, N + LAG):
                    if live(t):
                        n, k = t % N, t % 4
                        dve.wait_ge(s_gb, b * E + (t // NU + 1))
                        dve.wait_ge(s_hid, b * N + (t + 1))
                        v.tensor_tensor(hg[k][:, :], hid[k][:, :], gate_bank[n // NU % 2][:, :], ALU.mult).then_inc(s_hg, 1)
                    if t == N - 1 and end:
                        dve.wait_ge(s_ghi, m1 + 1)
                        v.tensor_tensor(row(gateT, m1)[LO:LO + E, :], gate_bank[0][0:E, :],
                                        row(gateT, m1)[0:E, :].bitcast(fp32), ALU.subtract).then_inc(s_glo, 1)
                    middle(t)
                    if live(t - 1) and (t - 1) % N not in POOL_STEPS:
                        k = (t - 1) % 4
                        dve.wait_ge(s_hghi, b * N + t)
                        v.tensor_tensor(hg_lo[k][:, :], hg[k][:, :], hg_hi[k][:, :].bitcast(fp32), ALU.subtract).then_inc(s_lo_dve, 1)
                    after(t)
                    if first and t == 6:
                        row_diag()
                    if first and t == 14:
                        row_weights()
                    if first and t == 10:
                        b2_parts()
                if start:
                    dve.wait_ge(s_pv, m2 + 1)
                    v.tensor_tensor(den[:, :], pv[:, :, DH], rms_inv[:, :], ALU.max).then_inc(s_den, 1)
                    dve.wait_ge(s_th, m2 + 1)
                    v.scalar_tensor_tensor(uh[:, :, :], th[:, :, :], 1.0, pv[:, :, 0:DH], ALU.add, ALU.mult)
                    dve.wait_ge(s_den, m2 * 2 + 1)
                    v.scalar_tensor_tensor(den[:, :], pv[:, :, DH], -1.0, den[:, :], ALU.mult, ALU.max).then_inc(s_den, 1)
                if live(N - 1):
                    dve.wait_ge(s_yT, b + 1)
                    v.tensor_tensor(row(x_all, b), row(x_all, b), bC[:, :], ALU.add).then_inc(s_o, 1)

            F0 = 8
            pv = bA[:, 0:NT * NS].rearrange("p (j n) -> p j n", j=NT)
            vz = bA[:, 0:NT * NZ].rearrange("p (j n) -> p j n", j=NT)
            iota_b = iota_e[:, :].unsqueeze(1).to_broadcast([P, NT, E])
            dve.wait_ge(s_bc, 80)
            dve.wait_ge(s_x_row1, 16)
            body(-2, False, True, True, lambda n: False, first=True)
            dve.wait_ge(s_x_rest, 16)
            body(-1, True, True, True, lambda n: n >= N)
            with dve.Fori(0, B - 3) as b:
                body(b, True, True, True, lambda n: True)
            last_turns(body)

        @block.tensor
        def _(pe):
            t_ = nc.tensor
            pe.wait_ge(s_const, 2)
            pe.wait_ge(s_small, 80)
            t_.transpose(bank[0][:, 0:R_END], small_rows[:, :], ident[0:R_END, 0:R_END]).then_inc(s_colsT, 1)
            pe.wait_ge(s_wqkvo, 80)
            t_.transpose(bank[1][:, 0:2 * DH], qk_raw[:, :], ident[:, :])
            t_.transpose(bank[2][:, 0:2 * DH], vo_raw[:, :], ident[:, :])
            t_.transpose(bank[3][0:DH, 0:D], wout_raw[:, :], ident[:, :]).then_inc(s_wT, 1)
            pe.wait_ge(s_silu, 1)
            pe.wait_ge(s_wmod, 16)
            for m in range(NMOD):
                last = t_.matmul(bank[4][:, m * B:(m + 1) * B], wmod_sb[:, m * D:(m + 1) * D], silu_c[:, :], start=True, stop=True)
            last.then_inc(s_mod, 1)
            pe.wait_ge(s_proj, 1)
            pe.wait_ge(s_const, CONSTS)

            def row_weights():
                pe.wait_ge(s_diag, 1)
                for n in range(2):
                    last = t_.matmul(bank[n][:, :], ones[:, :], diag_ga[:, 4 * n:4 * n + 4, :].rearrange("p b d -> p (b d)"),
                                     start=True, stop=True)
                last.then_inc(s_gab, 1)

            def scores(j, dst):
                t_.matmul(dst, kT[:, j * P:(j + 1) * P], qT[:, j * P:T], start=True, stop=True).then_inc(s_S, 1)

            def chain(b, end, start, t):
                m1, m2 = b + 1, b + 2
                if end:
                    if t == 4:
                        wait_apart(pe, s_hh, m1 + 1)
                        for j in range(NT):
                            last = t_.transpose(bB[0:DH, j * P:(j + 1) * P], hh[:, j, :], ident[:, :])
                        last.then_inc(s_hhT, 1)
                        dg = diag_ga[:, :, :].rearrange("p b d -> p (b d)")[:, bass.ds(m1 * D, D)]
                        for j in range(NT):
                            t_.matmul(bC[:, j * P:(j + 1) * P], hT[:, j * P:(j + 1) * P], dg, start=j == 0, stop=False,
                                      skip_group_check=True)
                    if t == 5:
                        wait_apart(pe, s_hhc, m1 + 1)
                        wg = wout_ga[:, :, :].rearrange("p b d -> p (b d)")[:, bass.ds(m1 * D, D)]
                        for j in range(NT):
                            last = t_.matmul(bC[:, j * P:(j + 1) * P], hhT[:, j * P:(j + 1) * P], wg, start=False, stop=j == NT - 1,
                                             skip_group_check=True)
                        last.then_inc(s_x1p, 1)
                if start:
                    if t == 4:
                        pe.wait_ge(s_xn[0], m2 + 1)
                        if end:
                            pe.wait_ge(s_den, m1 * 2 + 2)
                        for j in range(NT):
                            last = t_.transpose(bA[:, j * P:(j + 1) * P], xn[0][:, j, :], ident[:, :])
                        last.then_inc(s_xT, 1)
                    if t == 6:
                        pe.wait_ge(s_hT, m2 + 1)
                        t_.matmul(bB[:, :], wqk[:, :], hT[:, :], start=True, stop=True).then_inc(s_qk, 1)
                    if t == 7:
                        pe.wait_ge(s_sq, m2 + 1)
                        for j in range(NT):
                            last = t_.matmul(bA[:, j:j + 1], sq[:, j * P:(j + 1) * P], mean_col[:, :], start=True, stop=True)
                        last.then_inc(s_ms, 1)
                    if t == 8:
                        pe.wait_ge(s_qkT, m2 + 1)
                        for j in range(NT):
                            last = t_.matmul(bB[:, j * DH:(j + 1) * DH], hT[:, j * P:(j + 1) * P], wo[:, :], start=True, stop=True)
                        last.then_inc(s_ob, 1)
                        pe.wait_ge(s_mse, m2 + 1)
                        for j in range(NT):
                            last = t_.matmul(bA[:, j * NZ:(j + 1) * NZ], hT[:, j * P:(j + 1) * P], wvz[:, :], start=True, stop=True)
                        last.then_inc(s_vz, 1)
                if end:
                    if t == 9:
                        pe.wait_ge(s_xn[1], m1 + 1)
                        for j in range(NT):
                            last = t_.transpose(bC[:, j * P:(j + 1) * P], xn[1][:, j, :], ident[:, :])
                        last.then_inc(s_x2T, 1)
                    if t == 10:
                        pe.wait_ge(s_h2hi, m1 + 1)
                        for j in range(NT):
                            last = t_.matmul(bC[:, j * E:(j + 1) * E], h2T[:, j * P:(j + 1) * P], wr_sb[:, :], start=True, stop=True)
                        last.then_inc(s_lgp, 1)
                if start:
                    if t == 11:
                        pe.wait_ge(s_v, m2 + 1)
                        pe.wait_ge(s_z, m2 + 1)
                        F = bA[:, F0:F0 + NT]
                        t_.matmul(F, tri[:, :], zg[:, :, 1], start=True, stop=False, skip_group_check=True)
                        pe.wait_ge(s_zp, m2 + 1)
                        t_.matmul(F[:, 1:NT], ones[:, :], zp[:, :], start=False, stop=True, skip_group_check=True).then_inc(s_F, 1)
                    if t == 12:
                        pe.wait_ge(s_a, m2 + 1)
                        for j in range(NT):
                            last = t_.transpose(bA[0:1, j * P:(j + 1) * P], a_col[:, j:j + 1], ident[:, :])
                        last.then_inc(s_aT, 1)
                        if end:
                            pe.wait_ge(s_lg, m1 + 1)
                        scores(0, bC[:, 0:T])
                    if t == 13:
                        pe.wait_ge(s_zo, m2 + 1)
                        pe.wait_ge(s_M, m2 + 1)
                        t_.matmul(bB[:, :], ones[0:1, :], m_row[0:1, :], start=True, stop=True).then_inc(s_Mb, 1)
                    if t == 14:
                        scores(1, bA[:, 0:WIDTH[1]])
                        scores(3, bA[:, WIDTH[1]:T])
                    if t == 16:
                        wait_apart(pe, s_P, m2 * NT + 1)
                        scores(2, bC[:, 0:WIDTH[2]])
                    if t == 18:
                        pe.wait_ge(s_P, m2 * NT + NT)
                        for q in range(NT):
                            for j in range(q + 1):
                                o = START[j] + (q - j) * P
                                last = t_.matmul(bA[:, q * NS:(q + 1) * NS], ew[:, o:o + P], vs[:, j, :], start=j == 0, stop=j == q)
                        last.then_inc(s_pv, 1)

            def body(b, end, start, ahead, live, first=False, opening=False):
                for t in range(LAG, N + LAG):
                    if live(t):
                        n = t % N
                        e, u = divmod(n, NU)
                        own = b if t < N else b + 1
                        if opening and t == N:
                            pe.wait_ge(s_wlo, 2)
                            pe.wait_ge(s_h2lo, 1)
                        if t == N and not opening:
                            wait_apart(pe, s_h2lo, own + 1)
                        if not (opening and t < N + 2):
                            pe.wait_ge(s_hid, b * N + (t - 1))
                        w_hi, w_lo = (w[:, e, u * P:(u + 1) * P] for w in (w1_hi, w1_lo))
                        hx, hl, dst = row(h2_hi, own), row(h2_lo, own), up_bank[n % 2][:, :]
                        t_.matmul(dst, w_hi, hx, start=True, stop=False)
                        t_.matmul(dst, w_lo, hx, start=False, stop=False)
                        t_.matmul(dst, w_hi, hl, start=False, stop=True).then_inc(s_up, 1)
                    if t == N - 1 and end:
                        pe.wait_ge(s_gates, b + 2)
                        if live(N - 1):
                            wait_apart(pe, s_hg, b * N + (N - 2))
                        for k in range(NT):
                            last = t_.transpose(gate_bank[0][0:E, k * P:(k + 1) * P], gates[:, k, :], ident[:, :])
                        last.then_inc(s_gT, 1)
                    if live(t - LAG):
                        n, k = (t - LAG) % N, (t - LAG) % 4
                        e, u = divmod(n, NU)
                        w_hi, w_lo = w2_hi[:, e, u, :], w2_lo[:, e, u, :]
                        pe.wait_ge(s_hghi, b * N + (n + 1))
                        t_.matmul(y_bank[:, :], w_hi, hg_hi[k][:, :], start=n == 0, stop=False)
                        t_.matmul(y_bank[:, :], w_lo, hg_hi[k][:, :], start=False, stop=False)
                        if n == 0:
                            t_.matmul(y_bank[:, :], b2_hi[:, :], row(gateT, b), start=False, stop=False)
                            t_.matmul(y_bank[:, :], b2_lo[:, :], row(gateT, b), start=False, stop=False)
                        if n in POOL_STEPS:
                            pe.wait_ge(s_lo_pool, b * los(N - 1, True) + los(n, True))
                        else:
                            pe.wait_ge(s_lo_dve, b * los(N - 1, False) + los(n, False))
                        t_.matmul(y_bank[:, :], w_hi, hg_lo[k][:, :], start=False, stop=n == N - 1).then_inc(s_dn, 1)
                    if live(t) and t % NU == 0:
                        own, e = (b, t // NU) if t < N else (b + 1, t // NU - E)
                        if t == N:
                            wait_apart(pe, s_glo, own + 1)
                        elif not (opening and t < N + 3):
                            wait_apart(pe, s_hg, b * N + (t - 2))
                        t_.matmul(gate_bank[e % 2][:, :], sel_r[:, e, :], row(gateT, own), start=True, stop=True).then_inc(s_gb, 1)
                    chain(b, end, start, t)
                    if first and t == 9:
                        row_weights()
                if live(N - 1):
                    pe.wait_ge(s_ysb, b + 1)
                    for k in range(NT):
                        last = t_.transpose(bC[:, k * P:(k + 1) * P], y_sb[:, k * P:(k + 1) * P], ident[:, :])
                    last.then_inc(s_yT, 1)

            F0 = 8
            body(-2, False, True, True, lambda n: False, first=True)
            pe.wait_ge(s_wga, 2)
            pe.wait_ge(s_bc, 80)
            pe.wait_ge(s_sel, 2)
            pe.wait_ge(s_b2l, 1)
            body(-1, True, True, True, lambda n: n >= N, opening=True)
            with pe.Fori(0, B - 3) as b:
                body(b, True, True, True, lambda n: True)
            last_turns(body)


_INS = ["L0_attn_x", "L0_attn_norm_w", "L0_attn_Wq", "L0_attn_Wk", "L0_attn_Wv", "L0_attn_wi_w", "L0_attn_wi_b",
        "L0_attn_wf_w", "L0_attn_wf_b", "L0_attn_Wo", "L0_attn_bo", "L0_attn_Wout", "L0_ffn_Wr", "L0_ffn_br",
        "L0_ffn_W1", "L0_ffn_b1", "L0_ffn_W2", "L0_ffn_b2", "L0_c", "L0_wmod"]


def kernel(**inputs):
    import numpy as _np
    import concourse.bacc as _bacc
    from concourse import mybir as _mybir
    from concourse.bass_utils import run_bass_kernel_spmd as _run

    nc = _bacc.Bacc("TRN2", target_bir_lowering=False, num_devices=1)
    arrays, args = {}, []
    for name in _INS:
        a = _np.ascontiguousarray(inputs[name])
        arrays[f"in_{name}_dram"] = a
        args.append(nc.dram_tensor(f"in_{name}_dram", a.shape, _mybir.dt.from_np(a.dtype), kind="ExternalInput").ap())
    shape = inputs["L0_attn_x"].shape
    args.append(nc.dram_tensor("out_0_dram", shape, _mybir.dt.float32, kind="ExternalOutput").ap())
    adaln_mlstm_moe_kernel(nc, *args)
    r = _run(nc, [arrays], core_ids=[0])
    return r.results[0]["out_0_dram"]
```

```python
import concourse.bass as bass
from concourse import mybir
from contextlib import ExitStack


def adaln_mlstm_moe_kernel(
    nc: bass.Bass,
    x_in: bass.AP,
    norm_w: bass.AP,
    Wq: bass.AP,
    Wk: bass.AP,
    Wv: bass.AP,
    wi_w: bass.AP,
    wi_b: bass.AP,
    wf_w: bass.AP,
    wf_b: bass.AP,
    Wo: bass.AP,
    bo: bass.AP,
    Wout: bass.AP,
    Wr: bass.AP,
    br: bass.AP,
    W1: bass.AP,
    b1: bass.AP,
    W2: bass.AP,
    b2: bass.AP,
    c_in: bass.AP,
    wmod: bass.AP,
    out: bass.AP,
):
    fp32 = mybir.dt.float32
    fp32r = mybir.dt.float32r
    u32 = mybir.dt.uint32
    ALU = mybir.AluOpType
    ACT = mybir.ActivationFunctionType

    P = 128
    B, T, D = x_in.shape
    DH = Wq.shape[0]
    E = Wr.shape[1]
    FF = W1.shape[2]
    NT = T // P
    NU = FF // P
    N = E * NU
    LAG = 3
    NMOD = wmod.shape[1] // D
    LN_EPS, RMS_EPS = 1e-5, 1e-6
    SCALE = float(DH) ** -0.5
    FAR = 1e30
    NZ = DH + 2
    NVO = NZ + DH
    NS = DH + 1
    LO = 32
    GK = LO + E
    R_C, R_B1, R_WI, R_WF, R_NORM, R_END = 0, B, B + E * NU, B + E * NU + 1, B + E * NU + 2, B + E * NU + 3
    WIDTH = [T - P * j for j in range(NT)]
    START = [sum(WIDTH[:j]) for j in range(NT)]
    NW = sum(WIDTH)
    CONSTS = 8 + E
    POOL_STEPS = (1, 8, 9, 10, 11, 12, 13, 14, 15)
    LAST_STEPS = (1, 4, 6, 8, 10, 12)

    ctx = ExitStack()
    with ctx:
        def sb(name, shape, dt=fp32):
            return ctx.enter_context(nc.sbuf_tensor(name, shape, dt))

        def sem(name):
            return ctx.enter_context(nc.semaphore(name))

        ident = sb("ident", [P, P])
        ones = sb("ones", [P, P])
        tri = sb("tri", [P, P])
        far = sb("far", [P, P])
        mean_col = sb("mean_col", [P, 1])
        neg_row = sb("neg_row", [1, T])
        iota_e = sb("iota_e", [P, E])
        minus_half = sb("minus_half", [P, NT])
        sel_r = sb("sel_r", [GK, E, P], fp32r)
        small_rows = sb("small_rows", [R_END, D])
        qk_raw = sb("qk_raw", [2 * DH, D])
        vo_raw = sb("vo_raw", [2 * DH, D])
        wout_raw = sb("wout_raw", [D, DH])
        wmod_sb = sb("wmod_sb", [D, NMOD * D])
        w1_raw = sb("w1_raw", [D, E, FF])
        w2_raw = sb("w2_raw", [P, E, NU, D])
        b2_raw = sb("b2_raw", [GK, D])
        wr_sb = sb("wr_sb", [D, E])
        zb_bc = sb("zb_bc", [P, 2])
        bo_bc = sb("bo_bc", [P, DH])
        br_bc = sb("br_bc", [P, E])
        cols = sb("cols", [P, R_END])
        silu_c = sb("silu_c", [P, B])
        tanh_c = sb("tanh_c", [P, B])
        mods = sb("mods", [P, NMOD, B])
        sign_g = sb("sign_g", [P, 2, B])
        mag_g = sb("mag_g", [P, 2, B])
        wqk = sb("wqk", [D, 2 * DH])
        wvzo = sb("wvzo", [D, NVO])
        woutT = sb("woutT", [DH, D])
        diag_ga = sb("diag_ga", [P, B, D])
        wout_ga = sb("wout_ga", [DH, B, D])
        w1_hi = sb("w1_hi", [D, E, FF], fp32r)
        w1_lo = sb("w1_lo", [D, E, FF], fp32r)
        w2_hi = sb("w2_hi", [P, E, NU, D], fp32r)
        w2_lo = sb("w2_lo", [P, E, NU, D], fp32r)
        b2_hi = sb("b2_hi", [GK, D], fp32r)
        b2_lo = sb("b2_lo", [GK, D], fp32r)
        x_all = sb("x_all", [P, B * T])
        h2_hi = sb("h2_hi", [D, B * T], fp32r)
        h2_lo = sb("h2_lo", [D, B * T], fp32r)
        gateT = sb("gateT", [GK, B * T], fp32r)
        stats = [sb(f"stats{k}", [P, NT, 6]) for k in range(2)]
        mv = [sb(f"mv{k}", [P, NT, 2]) for k in range(2)]
        var_eps = [sb(f"var_eps{k}", [P, NT]) for k in range(2)]
        rstd = [sb(f"rstd{k}", [P, NT]) for k in range(2)]
        xn = [sb(f"xn{k}", [P, NT, D]) for k in range(2)]
        hT = sb("hT", [D, T])
        h_ga = sb("h_ga", [D, T])
        sq = sb("sq", [D, T])
        ms_eps = sb("ms_eps", [P, NT])
        rms = sb("rms", [P, NT])
        rms2 = sb("rms2", [P, NT])
        rms_inv = sb("rms_inv", [P, NT])
        kk = sb("kk", [2 * DH, T], fp32r)
        qq = sb("qq", [2 * DH, T], fp32r)
        qz = sb("qz", [2 * DH, T], fp32r)
        zg = sb("zg", [P, NT, 2])
        zp = sb("zp", [P, NT - 1])
        vs = sb("vs", [P, NT, NS])
        zo = sb("zo", [P, NT, DH])
        th = sb("th", [P, NT, DH])
        a_col = sb("a_col", [P, NT])
        m_row = sb("m_row", [1, T])
        mb = sb("mb", [P, NT, P])
        ew = sb("ew", [P, NW])
        den = sb("den", [P, NT])
        rden = sb("rden", [P, NT])
        uh = sb("uh", [P, NT, DH])
        hh = sb("hh", [P, NT, DH])
        hhT = sb("hhT", [DH, T])
        h2T = sb("h2T", [D, T])
        lg = sb("lg", [P, NT, E])
        mx = sb("mx", [P, NT, 8])
        ix = sb("ix", [P, NT, 8], u32)
        top_d = sb("top_d", [P, NT])
        top_e2 = sb("top_e2", [P, NT])
        top_s = sb("top_s", [P, NT])
        top_g = sb("top_g", [P, 2, NT])
        gate_a = sb("gate_a", [P, NT, E])
        gate_b = sb("gate_b", [P, NT, E])
        gates = sb("gates", [P, NT, E])
        hid = [sb(f"hid{k}", [P, T]) for k in range(4)]
        hg = [sb(f"hg{k}", [P, T]) for k in range(4)]
        hg_hi = [sb(f"hg_hi{k}", [P, T], fp32r) for k in range(4)]
        hg_lo = [sb(f"hg_lo{k}", [P, T], fp32r) for k in range(4)]
        y_sb = sb("y_sb", [D, T])
        sel = ew[0:GK, 0:E * P].rearrange("k (e m) -> k e m", e=E)

        bank = [ctx.enter_context(nc.psum_tensor(f"bank{k}", [P, 512], fp32)) for k in range(8)]
        up_bank, gate_bank, y_bank = bank[0:2], bank[2:4], bank[4]
        bA, bB, bC = bank[5], bank[6], bank[7]

        s_small = sem("s_small")
        s_wqko = sem("s_wqko")
        s_wvo = sem("s_wvo")
        s_wmod = sem("s_wmod")
        s_bc = sem("s_bc")
        s_w1 = sem("s_w1")
        s_w2 = sem("s_w2")
        s_b2 = sem("s_b2")
        s_x0 = sem("s_x0")
        s_x_row1 = sem("s_x_row1")
        s_x_rest = sem("s_x_rest")
        s_const = sem("s_const")
        s_pool = sem("s_pool")
        s_colsT = sem("s_colsT")
        s_wT = sem("s_wT")
        s_cols = sem("s_cols")
        s_tanhc = sem("s_tanhc")
        s_silu = sem("s_silu")
        s_mod = sem("s_mod")
        s_proj = sem("s_proj")
        s_dve0 = sem("s_dve0")
        s_mods = sem("s_mods")
        s_diag = sem("s_diag")
        s_gab = sem("s_gab")
        s_wga = sem("s_wga")
        s_sel0 = sem("s_sel0")
        s_sel = sem("s_sel")
        s_b2z = sem("s_b2z")
        s_b2h = sem("s_b2h")
        s_b2l = sem("s_b2l")
        s_whi = sem("s_whi")
        s_wlo = sem("s_wlo")
        s_st = [sem(f"s_st{k}") for k in range(2)]
        s_mv = [sem(f"s_mv{k}") for k in range(2)]
        s_ve = [sem(f"s_ve{k}") for k in range(2)]
        s_rs = [sem(f"s_rs{k}") for k in range(2)]
        s_xc = [sem(f"s_xc{k}") for k in range(2)]
        s_xn = [sem(f"s_xn{k}") for k in range(2)]
        s_xT = sem("s_xT")
        s_hT = sem("s_hT")
        s_sq = sem("s_sq")
        s_hga = sem("s_hga")
        s_qk = sem("s_qk")
        s_qkT = sem("s_qkT")
        s_kqlo = sem("s_kqlo")
        s_qz = sem("s_qz")
        s_ms = sem("s_ms")
        s_mse = sem("s_mse")
        s_rms = sem("s_rms")
        s_rms2 = sem("s_rms2")
        s_vz = sem("s_vz")
        s_z = sem("s_z")
        s_zp = sem("s_zp")
        s_v = sem("s_v")
        s_zo = sem("s_zo")
        s_th = sem("s_th")
        s_F = sem("s_F")
        s_a = sem("s_a")
        s_aT = sem("s_aT")
        s_M = sem("s_M")
        s_Mb = sem("s_Mb")
        s_mask = sem("s_mask")
        s_E = sem("s_E")
        s_S = sem("s_S")
        s_P = sem("s_P")
        s_pv = sem("s_pv")
        s_den = sem("s_den")
        s_rd = sem("s_rd")
        s_hh = sem("s_hh")
        s_hhT = sem("s_hhT")
        s_hhc = sem("s_hhc")
        s_x1p = sem("s_x1p")
        s_x1 = sem("s_x1")
        s_x2T = sem("s_x2T")
        s_h2 = sem("s_h2")
        s_h2hi = sem("s_h2hi")
        s_h2lo = sem("s_h2lo")
        s_lgp = sem("s_lgp")
        s_lg = sem("s_lg")
        s_mx = sem("s_mx")
        s_ix = sem("s_ix")
        s_td = sem("s_td")
        s_te = sem("s_te")
        s_ts = sem("s_ts")
        s_g1 = sem("s_g1")
        s_g2 = sem("s_g2")
        s_gab2 = sem("s_gab2")
        s_gates = sem("s_gates")
        s_gT = sem("s_gT")
        s_ghi = sem("s_ghi")
        s_glo = sem("s_glo")
        s_gb = sem("s_gb")
        s_up = sem("s_up")
        s_hid = sem("s_hid")
        s_hg = sem("s_hg")
        s_hghi = sem("s_hghi")
        s_lo_dve = sem("s_lo_dve")
        s_lo_pool = sem("s_lo_pool")
        s_dn = sem("s_dn")
        s_ysb = sem("s_ysb")
        s_yT = sem("s_yT")
        s_o = sem("s_o")
        s_out = sem("s_out")

        def vzo(j, start, stop):
            o = j % 2 * NVO
            return (bA, bB)[j // 2][:, o + start:o + stop]

        block = ctx.enter_context(nc.Block())

        x_v = x_in.rearrange("b (j p) d -> b p j d", p=P)
        out_v = out.rearrange("b (j p) d -> b p j d", p=P)

        def row(ap, b):
            return ap[:, bass.ds(b * T, T)]

        def bcast(ap, n):
            return ap.unsqueeze(2).to_broadcast([ap.shape[0], ap.shape[1], n])

        def wait_apart(eng, of, value):
            value = eng.to_reg(value)
            eng.wait_ge(s_const, CONSTS)
            eng.wait_ge(of, value)

        def pool_steps(live):
            return POOL_STEPS if live(N) else LAST_STEPS

        def los(n, by_pool, steps=POOL_STEPS):
            return sum(1 for m in range(n + 1) if (m % N in steps) == by_pool)

        def last_turns(body):
            body(B - 3, True, True, False, lambda n: True)
            body(B - 2, True, False, False, lambda n: True)
            body(B - 1, False, False, False, lambda n: n < N)

        @block.sync
        def _(sp):
            def load_x(b, n, of):
                sp.dma_start(x_all[:, b * T:(b + n) * T].rearrange("p (j d) -> p j d", j=n * NT),
                             x_v[b:b + n].rearrange("b p j d -> p b j d").rearrange("p b j d -> p (b j) d")).then_inc(of, 16)

            sp.dma_start(small_rows[R_C:R_C + B, :], c_in).then_inc(s_small, 16)
            sp.dma_start(small_rows[R_B1:R_WI, :], b1.rearrange("e (u f) -> (e u) f", f=P)).then_inc(s_small, 16)
            sp.dma_start(small_rows[R_WI:R_WF, :], wi_w).then_inc(s_small, 16)
            load_x(0, 1, s_x0)
            sp.dma_start(wout_raw[:, :], Wout).then_inc(s_wqko, 16)
            sp.dma_start(wmod_sb[:, :], wmod).then_inc(s_wmod, 16)
            load_x(1, 1, s_x_row1)
            sp.dma_start(wr_sb[:, :], Wr).then_inc(s_bc, 16)
            sp.dma_start(zb_bc[:, 0:1], wi_b.partition_broadcast(P)).then_inc(s_bc, 16)
            sp.dma_start(zb_bc[:, 1:2], wf_b.partition_broadcast(P)).then_inc(s_bc, 16)
            sp.dma_start(bo_bc[:, :], bo.partition_broadcast(P)).then_inc(s_bc, 16)
            sp.dma_start(br_bc[:, :], br.partition_broadcast(P)).then_inc(s_bc, 16)
            sp.dma_start(w1_raw[:, :, :], W1.rearrange("e h f -> h e f")).then_inc(s_w1, 16)
            sp.dma_start(w2_raw[:, :, :, :].rearrange("f e u h -> f (e u) h"),
                         W2.rearrange("e (u f) h -> f (e u) h", f=P)).then_inc(s_w2, 16)
            sp.dma_start(b2_raw[0:E, :], b2).then_inc(s_b2, 16)
            sp.dma_start(b2_raw[LO:LO + E, :], b2).then_inc(s_b2, 16)
            load_x(2, B - 2, s_x_rest)
            with sp.Fori(0, B) as b:
                sp.wait_ge(s_o, b + 1)
                sp.dma_start(out_v[bass.ds(b, 1)].rearrange("b p j d -> p (b j) d"),
                             row(x_all, b).rearrange("p (j d) -> p j d", j=NT)).then_inc(s_out, 16)
            sp.wait_ge(s_out, 16 * B)

        @block.gpsimd
        def _(pool):
            g = nc.gpsimd
            pool.dma_start(vo_raw[0:DH, :], Wv).then_inc(s_wvo, 16)
            pool.dma_start(vo_raw[DH:2 * DH, :], Wo).then_inc(s_wvo, 16)
            g.memset(ident[:, :], 0.0).then_inc(s_pool, 1)
            g.memset(tri[:, :], 1.0).then_inc(s_pool, 1)
            g.memset(far[:, :], 0.0).then_inc(s_pool, 1)
            g.memset(minus_half[:, :], -0.5).then_inc(s_const, 1)
            g.memset(qz[0:DH, :].bitcast(fp32), 0.0).then_inc(s_const, 1)
            pool.wait_ge(s_pool, 3)
            g.affine_select(out=ident[:, :], in_=ident[:, :], compare_op=ALU.not_equal, fill=1.0, base=0,
                            pattern=[[-1, P]], channel_multiplier=1).then_inc(s_const, 1)
            g.memset(ones[:, :], 1.0).then_inc(s_const, 1)
            g.memset(mean_col[:, :], 1.0 / D).then_inc(s_const, 1)
            g.memset(neg_row[:, :], -3e38).then_inc(s_const, 1)
            for e in range(E):
                g.memset(iota_e[:, e:e + 1], float(e)).then_inc(s_const, 1)
            g.affine_select(out=tri[:, :], in_=tri[:, :], compare_op=ALU.is_ge, fill=0.0, base=0,
                            pattern=[[1, P]], channel_multiplier=-1).then_inc(s_const, 1)
            g.affine_select(out=far[:, :], in_=far[:, :], compare_op=ALU.is_ge, fill=FAR, base=0,
                            pattern=[[1, P]], channel_multiplier=-1).then_inc(s_const, 1)
            pool.wait_ge(s_const, CONSTS)

            def norm(k, b, first=False):
                wait_apart(pool, s_mv[k], b + 1)
                g.tensor_scalar(var_eps[k][:, :], mv[k][:, :, 1], LN_EPS, None, ALU.add).then_inc(s_ve[k], 1)
                if k == 0 and not first:
                    wait_apart(pool, s_xT, b)
                g.tensor_tensor(xn[k][:, :, :], row(x_all, b).rearrange("p (j d) -> p j d", j=NT),
                                bcast(mv[k][:, :, 0], D), ALU.subtract).then_inc(s_xc[k], 1)
                pool.wait_ge(s_ve[k], b + 1)
                g.tensor_tensor(rstd[k][:, :], var_eps[k][:, :], minus_half[:, :], ALU.pow).then_inc(s_rs[k], 1)
                pool.wait_ge(s_xc[k], b + 1)
                wait_apart(pool, s_rs[k], b + 1)
                g.tensor_tensor(xn[k][:, :, :], xn[k][:, :, :], bcast(rstd[k][:, :], D), ALU.mult).then_inc(s_xn[k], 1)

            def body(b, end, start, ahead, live):
                m1, m2 = b + 1, b + 2
                for t in range(LAG, N + LAG):
                    if t == 7 and end:
                        norm(1, m1)
                    if t == 8 and start:
                        pool.wait_ge(s_mse, m2 + 1)
                        g.tensor_tensor(rms[:, :], ms_eps[:, :], minus_half[:, :], ALU.pow).then_inc(s_rms, 1)
                    if t == 5 and ahead:
                        norm(0, b + 3)
                    if t == 10 and end:
                        pool.wait_ge(s_h2, m1 + 1)
                        pool.wait_ge(s_h2hi, m1 + 1)
                        g.tensor_tensor(row(h2_lo, m1), h2T[:, :], row(h2_hi, m1).bitcast(fp32), ALU.subtract).then_inc(s_h2lo, 1)
                    if live(t - 1) and (t - 1) % N in pool_steps(live):
                        k = (t - 1) % 4
                        pool.wait_ge(s_hghi, b * N + t)
                        g.tensor_tensor(hg_lo[k][:, :], hg[k][:, :], hg_hi[k][:, :].bitcast(fp32), ALU.subtract).then_inc(s_lo_pool, 1)

            norm(0, 0, first=True)
            g.memset(sel, 0.0).then_inc(s_sel0, 1)
            pool.wait_ge(s_sel0, 1)
            g.affine_select(out=sel, in_=sel, compare_op=ALU.not_equal, fill=1.0, base=0,
                            pattern=[[-1, E], [0, P]], channel_multiplier=1).then_inc(s_sel0, 1)
            pool.wait_ge(s_sel0, 2)
            g.affine_select(out=sel, in_=sel, compare_op=ALU.not_equal, fill=1.0, base=-LO,
                            pattern=[[-1, E], [0, P]], channel_multiplier=1).then_inc(s_sel0, 1)
            body(-2, False, True, True, lambda n: False)
            g.memset(gateT[:, :].bitcast(fp32), 0.0).then_inc(s_sel, 1)
            pool.wait_ge(s_whi, 1)
            g.tensor_tensor(w1_lo[:, :, :], w1_raw[:, :, :], w1_hi[:, :, :].bitcast(fp32), ALU.subtract).then_inc(s_wlo, 1)
            pool.wait_ge(s_whi, 2)
            g.tensor_tensor(w2_lo[:, :, :, :], w2_raw[:, :, :, :], w2_hi[:, :, :, :].bitcast(fp32), ALU.subtract).then_inc(s_wlo, 1)
            body(-1, True, True, True, lambda n: n >= N)
            with pool.Fori(0, B - 3) as b:
                body(b, True, True, True, lambda n: True)
            last_turns(body)

        @block.scalar
        def _(act):
            a = nc.scalar
            act.dma_start(small_rows[R_WF:R_NORM, :], wf_w).then_inc(s_small, 16)
            act.dma_start(small_rows[R_NORM:R_END, :], norm_w.rearrange("(a n) -> a n", a=1)).then_inc(s_small, 16)
            act.dma_start(qk_raw[0:DH, :], Wq).then_inc(s_wqko, 16)
            act.dma_start(qk_raw[DH:2 * DH, :], Wk).then_inc(s_wqko, 16)
            act.wait_ge(s_cols, 1)
            a.activation(tanh_c[:, :], cols[:, R_C:R_C + B], ACT.Tanh, scale=0.5).then_inc(s_tanhc, 1)
            act.wait_ge(s_mods, 1)
            act.wait_ge(s_dve0, 3)

            def weights(p, j):
                last = a.activation(ew[:, START[j]:START[j] + P], mb[:, j, :], ACT.Exp, bias=a_col[:, j:j + 1], scale=-1.0)
                if j < NT - 1:
                    last = a.activation(ew[:, START[j] + P:START[j] + WIDTH[j]], bB[:, P * (j + 1):T],
                                        ACT.Exp, bias=a_col[:, j:j + 1], scale=-1.0)
                last.then_inc(s_E, 1)

            def body(b, end, start, ahead, live, weights_hi=False):
                m1, m2 = b + 1, b + 2
                for t in range(LAG, N + LAG):
                    if live(t):
                        n = t % N
                        act.wait_ge(s_up, b * N + (t + 1))
                        a.activation(hid[n % 4][:, :], up_bank[n % 2][:, :], ACT.Relu,
                                     bias=cols[:, R_B1 + n:R_B1 + n + 1]).then_inc(s_hid, 1)
                    if t == 10 and end:
                        a.activation(row(h2_hi, m1), bC[:, :], ACT.Identity, bias=mods[:, 3, bass.ds(m1, 1)],
                                     scale=mods[:, 4, bass.ds(m1, 1)]).then_inc(s_h2hi, 1)
                    if t == N - 1 and end:
                        act.wait_ge(s_gT, m1 + 1)
                        a.activation(row(gateT, m1)[0:E, :], gate_bank[0][0:E, :], ACT.Copy).then_inc(s_ghi, 1)
                    if t == 7 and start:
                        act.wait_ge(s_qk, m2 + 1)
                        a.activation(kk[DH:2 * DH, :], bB[DH:2 * DH, :], ACT.Copy)
                        a.activation(qq[0:DH, :], bB[0:DH, :], ACT.Copy).then_inc(s_qkT, 1)
                    if live(t - 1):
                        k = (t - 1) % 4
                        act.wait_ge(s_hg, b * N + t)
                        a.activation(hg_hi[k][:, :], hg[k][:, :], ACT.Copy).then_inc(s_hghi, 1)
                    if weights_hi and t == 7:
                        act.wait_ge(s_w1, 16)
                        a.activation(w1_hi[:, :, :], w1_raw[:, :, :], ACT.Copy).then_inc(s_whi, 1)
                        act.wait_ge(s_w2, 16)
                        a.activation(w2_hi[:, :, :, :], w2_raw[:, :, :, :], ACT.Copy).then_inc(s_whi, 1)
                    if t == 4 and end:
                        act.wait_ge(s_hhT, m1 + 1)
                        a.activation(hhT[:, :], bB[0:DH, :], ACT.Copy).then_inc(s_hhc, 1)
                    if t == 5 and start:
                        act.wait_ge(s_xT, m2 + 1)
                        a.activation(hT[:, :], bA[:, :], ACT.Identity, bias=mods[:, 0, bass.ds(m2, 1)],
                                     scale=mods[:, 1, bass.ds(m2, 1)]).then_inc(s_hT, 1)
                    if t == 6 and start:
                        a.activation(sq[:, :], bA[:, :], ACT.Square, bias=mods[:, 0, bass.ds(m2, 1)],
                                     scale=mods[:, 1, bass.ds(m2, 1)]).then_inc(s_sq, 1)
                    if t == 8 and start:
                        a.activation(h_ga[:, :], hT[:, :], ACT.Copy, scale=mods[:, 2, bass.ds(m2, 1)]).then_inc(s_hga, 1)
                    if t == 9 and end:
                        act.wait_ge(s_x2T, m1 + 1)
                        a.activation(h2T[:, :], bC[:, :], ACT.Identity, bias=mods[:, 3, bass.ds(m1, 1)],
                                     scale=mods[:, 4, bass.ds(m1, 1)]).then_inc(s_h2, 1)
                    if t == 10 and start:
                        act.wait_ge(s_zo, m2 + 1)
                        a.activation(th[:, :, :], zo[:, :, :], ACT.Tanh, scale=0.5).then_inc(s_th, 1)
                    if t == 12 and end:
                        act.wait_ge(s_td, m1 + 1)
                        a.activation(top_e2[:, :], top_d[:, :], ACT.Exp).then_inc(s_te, 1)
                    if start and t in (14, 15, 16):
                        if t == 14:
                            act.wait_ge(s_mask, m2 + 1)
                        if t == 16:
                            weights(m2, 3)
                        weights(m2, t - 14)
                if live(N - 1):
                    act.wait_ge(s_dn, b * N + N)
                    a.activation(y_sb[:, :], y_bank[:, :], ACT.Copy, scale=mods[:, 5, bass.ds(b, 1)]).then_inc(s_ysb, 1)

            body(-2, False, True, True, lambda n: False, weights_hi=True)
            body(-1, True, True, True, lambda n: n >= N)
            with act.Fori(0, B - 3) as b:
                body(b, True, True, True, lambda n: True)
            last_turns(body)

        @block.vector
        def _(dve):
            v = nc.vector

            def norm_stats(k, b):
                for j in range(NT):
                    last = v.bn_stats(stats[k][:, j, :], x_all[:, bass.ds(b * T + j * P, P)])
                last.then_inc(s_st[k], 1)

            def norm_aggr(k, b):
                wait_apart(dve, s_st[k], b + 1)
                for j in range(NT):
                    last = v.bn_aggr(mv[k][:, j, :], stats[k][:, j, :])
                last.then_inc(s_mv[k], 1)

            dve.wait_ge(s_colsT, 1)
            v.tensor_copy(cols[:, :], bank[0][:, 0:R_END]).then_inc(s_cols, 1)
            dve.wait_ge(s_tanhc, 1)
            v.scalar_tensor_tensor(silu_c[:, :], tanh_c[:, :], 1.0, cols[:, R_C:R_C + B], ALU.add, ALU.mult).then_inc(s_silu, 1)
            dve.wait_ge(s_x0, 16)
            norm_stats(0, 0)
            norm_aggr(0, 0)
            dve.wait_ge(s_wT, 1)
            nw = cols[:, R_NORM:R_NORM + 1]
            v.tensor_scalar(wqk[:, :], bank[1][:, 0:2 * DH], nw, SCALE, ALU.mult, ALU.mult)
            v.tensor_scalar(wvzo[:, 0:DH], bank[2][:, 0:DH], nw, None, ALU.mult)
            v.tensor_scalar(wvzo[:, DH:NZ], cols[:, R_WI:R_WF + 1], nw, None, ALU.mult)
            v.tensor_scalar(wvzo[:, NZ:NVO], bank[2][:, DH:2 * DH], nw, None, ALU.mult)
            v.tensor_copy(woutT[:, :], bank[3][0:DH, 0:D]).then_inc(s_proj, 1)
            dve.wait_ge(s_mod, 1)
            md = bank[4][:, 0:NMOD * B].rearrange("p (m b) -> p m b", m=NMOD)
            for m in (3, 0):
                v.tensor_scalar(mods[:, m, :], md[:, m, :], 0.5, None, ALU.mult)
                last = v.tensor_scalar(mods[:, m + 1, :], md[:, m + 1, :], 0.5, 1.0, ALU.mult, ALU.add)
            last.then_inc(s_mods, 1)
            for n, m in enumerate((2, 5)):
                v.tensor_scalar(sign_g[:, n, :], md[:, m, :], 0.0, 1.0, ALU.is_ge, ALU.mult)
                v.tensor_scalar(mods[:, m, :], md[:, m, :], 0.5, 0.25, ALU.mult, ALU.max)
                last = v.tensor_scalar(mag_g[:, n, :], md[:, m, :], -0.5, 0.25, ALU.mult, ALU.max)
            last.then_inc(s_dve0, 1)
            dve.wait_ge(s_dve0, 1)
            v.tensor_scalar(sign_g[:, :, :], sign_g[:, :, :], 2.0, -1.0, ALU.mult, ALU.add)
            v.tensor_tensor(mag_g[:, 0, :], mag_g[:, 0, :], mods[:, 2, :], ALU.max)
            v.tensor_tensor(mag_g[:, 1, :], mag_g[:, 1, :], mods[:, 5, :], ALU.max).then_inc(s_dve0, 1)
            dve.wait_ge(s_dve0, 2)
            v.tensor_tensor(mods[:, 2, :], sign_g[:, 0, :], mag_g[:, 0, :], ALU.mult)
            v.tensor_tensor(mods[:, 5, :], sign_g[:, 1, :], mag_g[:, 1, :], ALU.mult).then_inc(s_dve0, 1)
            dve.wait_ge(s_const, CONSTS)

            def row_diag():
                dve.wait_ge(s_dve0, 3)
                v.tensor_tensor(diag_ga[:, :, :], ident[:, :].unsqueeze(1).to_broadcast([P, B, D]),
                                bcast(mods[:, 2, :], D), ALU.mult).then_inc(s_diag, 1)

            def row_weights():
                dve.wait_ge(s_gab, 2)
                for n in range(2):
                    v.scalar_tensor_tensor(wout_ga[:, 4 * n:4 * n + 4, :],
                                           bank[n][0:DH, :].rearrange("p (b d) -> p b d", b=4), 0.5,
                                           woutT[:, :].unsqueeze(1).to_broadcast([DH, 4, D]),
                                           ALU.mult, ALU.mult).then_inc(s_wga, 1)

            def b2_parts():
                dve.wait_ge(s_sel0, 3)
                v.tensor_copy(sel_r[:, :, :], sel).then_inc(s_sel, 1)
                v.memset(b2_hi[:, :].bitcast(fp32), 0.0)
                v.memset(b2_lo[:, :].bitcast(fp32), 0.0).then_inc(s_b2z, 1)
                dve.wait_ge(s_b2z, 1)
                dve.wait_ge(s_b2, 32)
                v.tensor_copy(b2_hi[0:E, :], b2_raw[0:E, :])
                v.tensor_copy(b2_hi[LO:LO + E, :], b2_raw[LO:LO + E, :]).then_inc(s_b2h, 1)
                dve.wait_ge(s_b2h, 1)
                v.tensor_tensor(b2_lo[0:E, :], b2_raw[0:E, :], b2_hi[0:E, :].bitcast(fp32), ALU.subtract).then_inc(s_b2l, 1)

            def scores_times_weights(m, j):
                src = (bC[:, 0:T], bA[:, 0:WIDTH[1]], bC[:, 0:WIDTH[2]], bA[:, WIDTH[1]:T])[j]
                dve.wait_ge(s_E, m * NT + (1, 2, 4, 3)[j])
                dve.wait_ge(s_S, m * NT + (1, 3, 4, 3)[j])
                w = ew[:, START[j]:START[j] + WIDTH[j]]
                v.tensor_tensor(w, w, src, ALU.mult).then_inc(s_P, 1)

            def body(b, end, start, ahead, live, first=False):
                m1, m2 = b + 1, b + 2

                def middle(t):
                    if end:
                        if t == 3:
                            dve.wait_ge(s_den, m1 * 2 + 2)
                            v.reciprocal(rden[:, :], den[:, :]).then_inc(s_rd, 1)
                        if t == 6:
                            wait_apart(dve, s_x1, m1 + 1)
                            norm_stats(1, m1)
                        if t == 11:
                            dve.wait_ge(s_lgp, m1 + 1)
                            v.tensor_tensor(lg[:, :, :], bC[:, 0:NT * E].rearrange("p (j e) -> p j e", j=NT),
                                            br_bc[:, :].unsqueeze(1).to_broadcast([P, NT, E]), ALU.add).then_inc(s_lg, 1)
                        if t == 12:
                            dve.wait_ge(s_mx, m1 + 1)
                            v.tensor_tensor(top_d[:, :], mx[:, :, 1], mx[:, :, 0], ALU.subtract).then_inc(s_td, 1)
                            for j in range(NT):
                                last = v.max_index(ix[:, j, :], mx[:, j, :], lg[:, j, :])
                            last.then_inc(s_ix, 1)
                        if t == 13:
                            dve.wait_ge(s_te, m1 + 1)
                            v.tensor_scalar(top_s[:, :], top_e2[:, :], 1.0, None, ALU.add).then_inc(s_ts, 1)
                            dve.wait_ge(s_ix, m1 + 1)
                            v.tensor_tensor(gate_a[:, :, :], iota_b, ix[:, :, 0:1].to_broadcast([P, NT, E]), ALU.is_equal)
                            v.tensor_tensor(gate_b[:, :, :], iota_b, ix[:, :, 1:2].to_broadcast([P, NT, E]), ALU.is_equal)
                    if start:
                        if t == 7:
                            dve.wait_ge(s_qkT, m2 + 1)
                            v.tensor_tensor(kk[0:DH, :], bB[DH:2 * DH, :], kk[DH:2 * DH, :].bitcast(fp32), ALU.subtract)
                            v.tensor_tensor(qq[DH:2 * DH, :], bB[0:DH, :], qq[0:DH, :].bitcast(fp32), ALU.subtract).then_inc(s_kqlo, 1)
                        if t == 8:
                            v.tensor_copy(qz[DH:2 * DH, :], qq[0:DH, :]).then_inc(s_qz, 1)
                        if t == 9:
                            dve.wait_ge(s_rms, m2 + 1)
                            v.tensor_tensor(rms2[:, :], rms[:, :], rms[:, :], ALU.mult).then_inc(s_rms2, 1)
                            v.reciprocal(rms_inv[:, :], rms[:, :])
                            v.tensor_copy(vs[:, :, DH], rms[:, :])
                    if ahead and t == 4:
                        norm_stats(0, b + 3)

                def after(t):
                    if end:
                        if t == 3:
                            dve.wait_ge(s_rd, m1 + 1)
                            v.tensor_tensor(hh[:, :, :], uh[:, :, :], bcast(rden[:, :], DH), ALU.mult).then_inc(s_hh, 1)
                        if t == 5:
                            dve.wait_ge(s_x1p, m1 + 1)
                            v.tensor_tensor(row(x_all, m1), row(x_all, m1), bC[:, :], ALU.add).then_inc(s_x1, 1)
                        if t == 6:
                            norm_aggr(1, m1)
                        if t == 11:
                            wait_apart(dve, s_lg, m1 + 1)
                            for j in range(NT):
                                last = v.max(mx[:, j, :], lg[:, j, :])
                            last.then_inc(s_mx, 1)
                        if t == 13:
                            dve.wait_ge(s_ts, m1 + 1)
                            v.reciprocal(top_g[:, 0, :], top_s[:, :]).then_inc(s_g1, 1)
                    if end and t == 13:
                        dve.wait_ge(s_g1, m1 + 1)
                        v.tensor_tensor(top_g[:, 1, :], top_g[:, 0, :], top_e2[:, :], ALU.mult).then_inc(s_g2, 1)
                        v.tensor_tensor(gate_a[:, :, :], gate_a[:, :, :], bcast(top_g[:, 0, :], E), ALU.mult)
                        dve.wait_ge(s_g2, m1 + 1)
                        v.tensor_tensor(gate_b[:, :, :], gate_b[:, :, :], bcast(top_g[:, 1, :], E), ALU.mult).then_inc(s_gab2, 1)
                        dve.wait_ge(s_gab2, m1 + 1)
                        v.tensor_tensor(gates[:, :, :], gate_a[:, :, :], gate_b[:, :, :], ALU.add).then_inc(s_gates, 1)
                    if start:
                        if t == 7:
                            dve.wait_ge(s_ms, m2 + 1)
                            v.tensor_scalar(ms_eps[:, :], bA[:, 0:NT], RMS_EPS, None, ALU.add).then_inc(s_mse, 1)
                        if t == 9:
                            dve.wait_ge(s_vz, m2 + 1)
                            for j in range(NT):
                                last = v.scalar_tensor_tensor(zo[:, j, :], vzo(j, NZ, NVO), rms[:, j:j + 1],
                                                              bo_bc[:, :], ALU.mult, ALU.add)
                            last.then_inc(s_zo, 1)
                            dve.wait_ge(s_vz, m2 + 1)
                            for j in range(NT):
                                last = v.scalar_tensor_tensor(zg[:, j, :], vzo(j, DH, NZ), rms[:, j:j + 1],
                                                              zb_bc[:, :], ALU.mult, ALU.add)
                            last.then_inc(s_z, 1)
                            wait_apart(dve, s_z, m2 + 1)
                            v.tensor_tensor_scan(zp[:, :], ones[:, 0:NT - 1], zg[:, 0:NT - 1, 1], 0.0, ALU.mult, ALU.add).then_inc(s_zp, 1)
                            dve.wait_ge(s_rms2, m2 + 1)
                            for h in range(2):
                                last = v.tensor_tensor(vs[:, 2 * h:2 * h + 2, 0:DH], vz[h][:, :, 0:DH],
                                                       bcast(rms2[:, 2 * h:2 * h + 2], DH), ALU.mult)
                            last.then_inc(s_v, 1)
                        if t == 11:
                            dve.wait_ge(s_F, m2 + 1)
                            v.tensor_tensor(a_col[:, :], zg[:, :, 0], bA[:, F0:F0 + NT], ALU.subtract).then_inc(s_a, 1)
                        if t == 12:
                            dve.wait_ge(s_aT, m2 + 1)
                            v.tensor_tensor_scan(m_row[0:1, :], bA[0:1, :], neg_row[0:1, :], -3e38, ALU.max, ALU.max).then_inc(s_M, 1)
                        if t == 13:
                            dve.wait_ge(s_Mb, m2 + 1)
                            v.tensor_tensor(mb[:, :, :], bB[:, :].rearrange("p (j t) -> p j t", j=NT),
                                            far[:, :].unsqueeze(1).to_broadcast([P, NT, P]), ALU.add).then_inc(s_mask, 1)
                        if t in (14, 15):
                            scores_times_weights(m2, t - 14)
                        if t == 16:
                            scores_times_weights(m2, 3)
                            scores_times_weights(m2, 2)
                    if ahead and t == 4:
                        if first:
                            dve.wait_ge(s_xn[0], 1)
                        norm_aggr(0, b + 3)

                for t in range(LAG, N + LAG):
                    if live(t):
                        n, k = t % N, t % 4
                        dve.wait_ge(s_gb, b * E + (t // NU + 1))
                        dve.wait_ge(s_hid, b * N + (t + 1))
                        v.tensor_tensor(hg[k][:, :], hid[k][:, :], gate_bank[n // NU % 2][:, :], ALU.mult).then_inc(s_hg, 1)
                    if t == N - 1 and end:
                        dve.wait_ge(s_ghi, m1 + 1)
                        v.tensor_tensor(row(gateT, m1)[LO:LO + E, :], gate_bank[0][0:E, :],
                                        row(gateT, m1)[0:E, :].bitcast(fp32), ALU.subtract).then_inc(s_glo, 1)
                    middle(t)
                    if live(t - 1) and (t - 1) % N not in pool_steps(live):
                        k = (t - 1) % 4
                        dve.wait_ge(s_hghi, b * N + t)
                        v.tensor_tensor(hg_lo[k][:, :], hg[k][:, :], hg_hi[k][:, :].bitcast(fp32), ALU.subtract).then_inc(s_lo_dve, 1)
                    after(t)
                    if first and t == 6:
                        row_diag()
                    if first and t == 17:
                        row_weights()
                    if first and t == 10:
                        b2_parts()
                if start:
                    dve.wait_ge(s_pv, m2 + 1)
                    v.tensor_tensor(den[:, :], pv[:, :, DH], rms_inv[:, :], ALU.max).then_inc(s_den, 1)
                    dve.wait_ge(s_th, m2 + 1)
                    v.scalar_tensor_tensor(uh[:, :, :], th[:, :, :], 1.0, pv[:, :, 0:DH], ALU.add, ALU.mult)
                    dve.wait_ge(s_den, m2 * 2 + 1)
                    v.scalar_tensor_tensor(den[:, :], pv[:, :, DH], -1.0, den[:, :], ALU.mult, ALU.max).then_inc(s_den, 1)
                if live(N - 1):
                    dve.wait_ge(s_yT, b + 1)
                    v.tensor_tensor(row(x_all, b), row(x_all, b), bC[:, :], ALU.add).then_inc(s_o, 1)

            F0 = 8
            pv = bA[:, 0:NT * NS].rearrange("p (j n) -> p j n", j=NT)
            vz = [k[:, 0:2 * NVO].rearrange("p (j n) -> p j n", j=2) for k in (bA, bB)]
            iota_b = iota_e[:, :].unsqueeze(1).to_broadcast([P, NT, E])
            dve.wait_ge(s_bc, 80)
            dve.wait_ge(s_x_row1, 16)
            body(-2, False, True, True, lambda n: False, first=True)
            dve.wait_ge(s_x_rest, 16)
            body(-1, True, True, True, lambda n: n >= N)
            with dve.Fori(0, B - 3) as b:
                body(b, True, True, True, lambda n: True)
            last_turns(body)

        @block.tensor
        def _(pe):
            t_ = nc.tensor
            pe.wait_ge(s_const, 3)
            pe.wait_ge(s_small, 80)
            t_.transpose(bank[0][:, 0:R_END], small_rows[:, :], ident[0:R_END, 0:R_END]).then_inc(s_colsT, 1)
            pe.wait_ge(s_wqko, 48)
            pe.wait_ge(s_wvo, 32)
            t_.transpose(bank[1][:, 0:2 * DH], qk_raw[:, :], ident[:, :])
            t_.transpose(bank[2][:, 0:2 * DH], vo_raw[:, :], ident[:, :])
            t_.transpose(bank[3][0:DH, 0:D], wout_raw[:, :], ident[:, :]).then_inc(s_wT, 1)
            pe.wait_ge(s_silu, 1)
            pe.wait_ge(s_wmod, 16)
            for m in range(NMOD):
                last = t_.matmul(bank[4][:, m * B:(m + 1) * B], wmod_sb[:, m * D:(m + 1) * D], silu_c[:, :], start=True, stop=True)
            last.then_inc(s_mod, 1)
            pe.wait_ge(s_proj, 1)
            pe.wait_ge(s_const, CONSTS)

            def row_weights(n):
                pe.wait_ge(s_diag, 1)
                t_.matmul(bank[n][:, :], ones[:, :], diag_ga[:, 4 * n:4 * n + 4, :].rearrange("p b d -> p (b d)"),
                          start=True, stop=True).then_inc(s_gab, 1)

            def scores(j, dst):
                t_.matmul(dst, kk[:, j * P:(j + 1) * P], qq[:, j * P:T], start=True, stop=False)
                t_.matmul(dst, kk[:, j * P:(j + 1) * P], qz[:, j * P:T], start=False, stop=True).then_inc(s_S, 1)

            def chain(b, end, start, t):
                m1, m2 = b + 1, b + 2
                if end:
                    if t == 4:
                        pe.wait_ge(s_hga, m1 + 1)
                        pe.wait_ge(s_rd, m1 + 1)
                        for j in range(NT):
                            t_.matmul(bC[:, j * P:(j + 1) * P], h_ga[:, j * P:(j + 1) * P], ident[:, :], start=j == 0, stop=False,
                                      is_transpose=True, skip_group_check=True)
                        wait_apart(pe, s_hh, m1 + 1)
                        for j in range(NT):
                            last = t_.transpose(bB[0:DH, j * P:(j + 1) * P], hh[:, j, :], ident[:, :])
                        last.then_inc(s_hhT, 1)
                    if t == 5:
                        wait_apart(pe, s_hhc, m1 + 1)
                        wg = wout_ga[:, :, :].rearrange("p b d -> p (b d)")[:, bass.ds(m1 * D, D)]
                        for j in range(NT):
                            last = t_.matmul(bC[:, j * P:(j + 1) * P], hhT[:, j * P:(j + 1) * P], wg, start=False, stop=j == NT - 1,
                                             skip_group_check=True)
                        last.then_inc(s_x1p, 1)
                if start:
                    if t == 4:
                        pe.wait_ge(s_xn[0], m2 + 1)
                        if end:
                            pe.wait_ge(s_den, m1 * 2 + 2)
                        for j in range(NT):
                            last = t_.transpose(bA[:, j * P:(j + 1) * P], xn[0][:, j, :], ident[:, :])
                        last.then_inc(s_xT, 1)
                    if t == 6:
                        pe.wait_ge(s_hT, m2 + 1)
                        t_.matmul(bB[:, :], wqk[:, :], hT[:, :], start=True, stop=True).then_inc(s_qk, 1)
                    if t == 7:
                        pe.wait_ge(s_sq, m2 + 1)
                        for j in range(NT):
                            last = t_.matmul(bA[:, j:j + 1], sq[:, j * P:(j + 1) * P], mean_col[:, :], start=True, stop=True)
                        last.then_inc(s_ms, 1)
                if end:
                    if t == 9:
                        pe.wait_ge(s_xn[1], m1 + 1)
                        for j in range(NT):
                            last = t_.transpose(bC[:, j * P:(j + 1) * P], xn[1][:, j, :], ident[:, :])
                        last.then_inc(s_x2T, 1)
                if start:
                    if t == 11:
                        pe.wait_ge(s_v, m2 + 1)
                        pe.wait_ge(s_z, m2 + 1)
                        pe.wait_ge(s_zo, m2 + 1)
                        F = bA[:, F0:F0 + NT]
                        t_.matmul(F, tri[:, :], zg[:, :, 1], start=True, stop=False, skip_group_check=True)
                        pe.wait_ge(s_zp, m2 + 1)
                        t_.matmul(F[:, 1:NT], ones[:, :], zp[:, :], start=False, stop=True, skip_group_check=True).then_inc(s_F, 1)
                    if t == 12:
                        pe.wait_ge(s_a, m2 + 1)
                        for j in range(NT):
                            last = t_.transpose(bA[0:1, j * P:(j + 1) * P], a_col[:, j:j + 1], ident[:, :])
                        last.then_inc(s_aT, 1)
                        if end:
                            pe.wait_ge(s_lg, m1 + 1)
                        pe.wait_ge(s_qz, m2 + 1)
                        scores(0, bC[:, 0:T])
                    if t == 13:
                        pe.wait_ge(s_zo, m2 + 1)
                        pe.wait_ge(s_M, m2 + 1)
                        t_.matmul(bB[:, :], ones[0:1, :], m_row[0:1, :], start=True, stop=True).then_inc(s_Mb, 1)
                    if t == 14:
                        scores(1, bA[:, 0:WIDTH[1]])
                        scores(3, bA[:, WIDTH[1]:T])
                    if t == 16:
                        wait_apart(pe, s_P, m2 * NT + 1)
                        scores(2, bC[:, 0:WIDTH[2]])
                    if t == 18:
                        pe.wait_ge(s_P, m2 * NT + NT)
                        for q in range(NT):
                            for j in range(q + 1):
                                o = START[j] + (q - j) * P
                                last = t_.matmul(bA[:, q * NS:(q + 1) * NS], ew[:, o:o + P], vs[:, j, :], start=j == 0, stop=j == q)
                        last.then_inc(s_pv, 1)

            def keep_busy(n):
                for _ in range(n):
                    t_.matmul(bank[3][:, 0:P], ident[:, :], ones[:, :], start=True, stop=True)

            def body(b, end, start, ahead, live, first=False, opening=False):
                for t in range(LAG, N + LAG):
                    if first and t > LAG or opening and t < N - 1:
                        keep_busy(2)
                    if opening and t == 5:
                        pe.wait_ge(s_wga, 2)
                    if live(t):
                        n = t % N
                        e, u = divmod(n, NU)
                        own = b if t < N else b + 1
                        if opening and t == N:
                            pe.wait_ge(s_wlo, 2)
                            pe.wait_ge(s_h2lo, 1)
                        if t == N and not opening:
                            wait_apart(pe, s_h2lo, own + 1)
                        if not (opening and t < N + 2):
                            pe.wait_ge(s_hid, b * N + (t - 1))
                        w_hi, w_lo = (w[:, e, u * P:(u + 1) * P] for w in (w1_hi, w1_lo))
                        hx, hl, dst = row(h2_hi, own), row(h2_lo, own), up_bank[n % 2][:, :]
                        t_.matmul(dst, w_hi, hx, start=True, stop=False)
                        t_.matmul(dst, w_lo, hx, start=False, stop=False)
                        t_.matmul(dst, w_hi, hl, start=False, stop=True).then_inc(s_up, 1)
                    if t == (N - 2 if opening else N - 1) and end:
                        pe.wait_ge(s_gates, b + 2)
                        if live(N - 1):
                            wait_apart(pe, s_hg, b * N + (N - 2))
                        for k in range(NT):
                            last = t_.transpose(gate_bank[0][0:E, k * P:(k + 1) * P], gates[:, k, :], ident[:, :])
                        last.then_inc(s_gT, 1)
                    if live(t - LAG):
                        n, k = (t - LAG) % N, (t - LAG) % 4
                        e, u = divmod(n, NU)
                        w_hi, w_lo = w2_hi[:, e, u, :], w2_lo[:, e, u, :]
                        pe.wait_ge(s_hghi, b * N + (n + 1))
                        t_.matmul(y_bank[:, :], w_hi, hg_hi[k][:, :], start=n == 0, stop=False)
                        t_.matmul(y_bank[:, :], w_lo, hg_hi[k][:, :], start=False, stop=False)
                        if n == 0:
                            t_.matmul(y_bank[:, :], b2_hi[:, :], row(gateT, b), start=False, stop=False)
                            t_.matmul(y_bank[:, :], b2_lo[:, :], row(gateT, b), start=False, stop=False)
                        if n in pool_steps(live):
                            pe.wait_ge(s_lo_pool, b * los(N - 1, True) + los(n, True, pool_steps(live)))
                        else:
                            pe.wait_ge(s_lo_dve, b * los(N - 1, False) + los(n, False, pool_steps(live)))
                        t_.matmul(y_bank[:, :], w_hi, hg_lo[k][:, :], start=False, stop=n == N - 1).then_inc(s_dn, 1)
                    if live(t) and t % NU == 0:
                        own, e = (b, t // NU) if t < N else (b + 1, t // NU - E)
                        if t == N:
                            wait_apart(pe, s_glo, own + 1)
                        elif not (opening and t < N + 3):
                            wait_apart(pe, s_hg, b * N + (t - 2))
                        t_.matmul(gate_bank[e % 2][:, :], sel_r[:, e, :], row(gateT, own), start=True, stop=True).then_inc(s_gb, 1)
                    if t == 9 and start:
                        wait_apart(pe, s_kqlo, b + 3)
                        pe.wait_ge(s_mse, b + 3)
                        for j in range(NT):
                            last = t_.matmul(vzo(j, 0, NVO), hT[:, j * P:(j + 1) * P], wvzo[:, :], start=True, stop=True)
                        last.then_inc(s_vz, 1)
                    if t == 11 and end:
                        pe.wait_ge(s_h2hi, b + 2)
                        for j in range(NT):
                            last = t_.matmul(bC[:, j * E:(j + 1) * E], h2T[:, j * P:(j + 1) * P], wr_sb[:, :], start=True, stop=True)
                        last.then_inc(s_lgp, 1)
                    chain(b, end, start, t)
                    if first and t in (8, 10):
                        row_weights((t - 8) // 2)
                if live(N - 1):
                    pe.wait_ge(s_ysb, b + 1)
                    for k in range(NT):
                        last = t_.transpose(bC[:, k * P:(k + 1) * P], y_sb[:, k * P:(k + 1) * P], ident[:, :])
                    last.then_inc(s_yT, 1)

            F0 = 8
            body(-2, False, True, True, lambda n: False, first=True)
            pe.wait_ge(s_bc, 80)
            pe.wait_ge(s_sel, 2)
            pe.wait_ge(s_b2l, 1)
            body(-1, True, True, True, lambda n: n >= N, opening=True)
            with pe.Fori(0, B - 3) as b:
                body(b, True, True, True, lambda n: True)
            last_turns(body)


_INS = ["L0_attn_x", "L0_attn_norm_w", "L0_attn_Wq", "L0_attn_Wk", "L0_attn_Wv", "L0_attn_wi_w", "L0_attn_wi_b",
        "L0_attn_wf_w", "L0_attn_wf_b", "L0_attn_Wo", "L0_attn_bo", "L0_attn_Wout", "L0_ffn_Wr", "L0_ffn_br",
        "L0_ffn_W1", "L0_ffn_b1", "L0_ffn_W2", "L0_ffn_b2", "L0_c", "L0_wmod"]


def kernel(**inputs):
    import numpy as _np
    import concourse.bacc as _bacc
    from concourse import mybir as _mybir
    from concourse.bass_utils import run_bass_kernel_spmd as _run

    nc = _bacc.Bacc("TRN2", target_bir_lowering=False, num_devices=1)
    arrays, args = {}, []
    for name in _INS:
        a = _np.ascontiguousarray(inputs[name])
        arrays[f"in_{name}_dram"] = a
        args.append(nc.dram_tensor(f"in_{name}_dram", a.shape, _mybir.dt.from_np(a.dtype), kind="ExternalInput").ap())
    shape = inputs["L0_attn_x"].shape
    args.append(nc.dram_tensor("out_0_dram", shape, _mybir.dt.float32, kind="ExternalOutput").ap())
    adaln_mlstm_moe_kernel(nc, *args)
    r = _run(nc, [arrays], core_ids=[0])
    return r.results[0]["out_0_dram"]
```
